# Optimizing a Trainium2 kernel written in Bass

```python
import numpy as np
import jax
import jax.numpy as jnp

def _softmax(x, axis=-1):
    return jax.nn.softmax(x, axis=axis)

def _gelu(x):
    return jax.nn.gelu(x, approximate=True)

def _silu(x):
    return jax.nn.silu(x)

def _sigmoid(x):
    return jax.nn.sigmoid(x)

def _layernorm(x, axis=-1, eps=1e-05):
    m = jnp.mean(x, axis=axis, keepdims=True)
    v = jnp.var(x, axis=axis, keepdims=True)
    return (x - m) / jnp.sqrt(v + eps)

def _scatter_add(tgt, idx, src, axis=0):
    return tgt.at[idx].add(src)

def _segment_sum(src, seg, n):
    return jax.ops.segment_sum(src, seg, n)
kernel_name = 'mk_decoder_preln_d1_seqx_r8_d7824b'

def setup_inputs(seed: int=0):
    np.random.seed(seed)
    _w = jnp.asarray

    def _rec_inputs():
        import jax
        import jax.numpy as jnp
        _rk = jax.random.key(seed)
        x = -0.0002928 + 1 * jax.random.normal(jax.random.fold_in(_rk, 1), (16, 128, 128), jnp.float32)
        _lenS = 128 - jax.random.randint(jax.random.fold_in(_rk, 7), (16,), 0, max(1, 128 // 4) + 1, jnp.int32)
        _lenS2 = 128 - jax.random.randint(jax.random.fold_in(_rk, 8), (16,), 0, max(1, 128 // 4) + 1, jnp.int32)
        _ctx_1024P = jax.random.normal(jax.random.fold_in(_rk, 11), (16, 16, 128), jnp.float32)
        _ctx_1024c = jax.random.dirichlet(jax.random.fold_in(_rk, 511), 0.3 * jnp.ones((16,), jnp.float32), (16, 128))
        _ctx_1024t = jnp.einsum('bsk,bkd->bsd', _ctx_1024c, _ctx_1024P)
        _ctx_1024t = _ctx_1024t * jax.lax.rsqrt(jnp.mean(jnp.square(_ctx_1024t)) + 1e-12) * 0.953939
        ctx_1024 = -1.39393e-06 + 0.999914 * (_ctx_1024t + 0.3 * jax.random.normal(jax.random.fold_in(_rk, 611), (16, 128, 128), jnp.float32))
        return (x, ctx_1024)
    x, ctx_1024 = _rec_inputs()

    def _L0_attn_setup():
        import jax, jax.numpy as jnp
        import numpy as np
        B, S, IN_DIM, D_MODEL, NUM_HEADS = (4, 256, 128, 128, 16)
        HEAD_DIM = D_MODEL // NUM_HEADS
        CAUSAL = True
        NEG = -9000000000000000.0

        def _xavier(key, shape):
            fan_out, fan_in = shape
            limit = (6.0 / (fan_in + fan_out)) ** 0.5
            return jax.random.uniform(key, shape, jnp.float32, -limit, limit)
        key = jax.random.key(seed)
        ks = jax.random.split(key, 5)
        x = jax.random.normal(ks[0], (B, S, IN_DIM), jnp.float32)
        Wq = _xavier(ks[1], (D_MODEL, IN_DIM))
        Wk = _xavier(ks[2], (D_MODEL, IN_DIM))
        Wv = _xavier(ks[3], (D_MODEL, IN_DIM))
        Wo = _xavier(ks[4], (D_MODEL, D_MODEL))
        bq = jnp.zeros((D_MODEL,), jnp.float32)
        bk = jnp.zeros((D_MODEL,), jnp.float32)
        bv = jnp.zeros((D_MODEL,), jnp.float32)
        bo = jnp.zeros((D_MODEL,), jnp.float32)
        return {'x': x, 'Wq': Wq, 'bq': bq, 'Wk': Wk, 'bk': bk, 'Wv': Wv, 'bv': bv, 'Wo': Wo, 'bo': bo}
    _L0_attn_all = _L0_attn_setup()
    _L0_attn_in = {k: v for k, v in _L0_attn_all.items() if k in ('Wq', 'bq', 'Wk', 'bk', 'Wv', 'bv', 'Wo', 'bo')}
    del _L0_attn_all

    def _L0_xattn_setup():
        import jax, jax.numpy as jnp
        import numpy as np
        EMBED_PHI = 128
        EMBED_F = 128
        HIDDEN_F = 128
        N_HEADS = 16
        B, S = (2, 256)
        key = jax.random.key(seed)
        ks = jax.random.split(key, 9)
        sphi = 1.0 / np.sqrt(EMBED_PHI)
        sf = 1.0 / np.sqrt(EMBED_F)
        sh = 1.0 / np.sqrt(HIDDEN_F)
        return {'q': jax.random.normal(ks[0], (B, S, EMBED_PHI), jnp.float32), 'k': jax.random.normal(ks[1], (B, S, EMBED_PHI), jnp.float32), 'v': jax.random.normal(ks[2], (B, S, EMBED_F), jnp.float32), 'Wq': jax.random.normal(ks[3], (HIDDEN_F, EMBED_PHI), jnp.float32) * sphi, 'Wk': jax.random.normal(ks[4], (HIDDEN_F, EMBED_PHI), jnp.float32) * sphi, 'Wv': jax.random.normal(ks[5], (HIDDEN_F, EMBED_F), jnp.float32) * sf, 'bv': jax.random.normal(ks[6], (HIDDEN_F,), jnp.float32) * sf, 'Wo': jax.random.normal(ks[7], (EMBED_F, HIDDEN_F), jnp.float32) * sh, 'bo': jax.random.normal(ks[8], (EMBED_F,), jnp.float32) * sh}
    _L0_xattn_all = _L0_xattn_setup()
    _L0_xattn_in = {k: v for k, v in _L0_xattn_all.items() if k in ('Wq', 'Wk', 'Wv', 'bv', 'Wo', 'bo')}
    del _L0_xattn_all

    def _L0_ffn_setup():
        import jax, jax.numpy as jnp
        import numpy as np
        import math
        B, S, D = (4, 256, 128)
        E, DFF = (16, 256)
        CAP_FACTOR = 2.0
        ROUTER_HIDDEN = 128
        CAPACITY = int(math.ceil(S * CAP_FACTOR / E))
        key = jax.random.key(seed)
        ks = jax.random.split(key, 6)

        def uinit(k, shape, fan_in):
            bound = math.sqrt(3.0) * math.sqrt(1.0 / 3.0) / math.sqrt(fan_in)
            return jax.random.uniform(k, shape, jnp.float32, -bound, bound)
        return {'hidden_states': jax.random.normal(ks[0], (B, S, D), jnp.float32), 'router_w1': jax.random.normal(ks[1], (D, ROUTER_HIDDEN), jnp.float32) / math.sqrt(D), 'router_w2': jax.random.normal(ks[2], (ROUTER_HIDDEN, E), jnp.float32) / math.sqrt(ROUTER_HIDDEN), 'w1': uinit(ks[3], (E, D, DFF), D), 'w2': uinit(ks[4], (E, D, DFF), D), 'w3': uinit(ks[5], (E, DFF, D), DFF)}
    _L0_ffn_all = _L0_ffn_setup()
    _L0_ffn_in = {k: v for k, v in _L0_ffn_all.items() if k in ('router_w1', 'router_w2', 'w1', 'w2', 'w3')}
    del _L0_ffn_all
    return {'x': x, 'ctx_1024': ctx_1024, 'L0_attn_Wq': _L0_attn_in['Wq'], 'L0_attn_bq': _L0_attn_in['bq'], 'L0_attn_Wk': _L0_attn_in['Wk'], 'L0_attn_bk': _L0_attn_in['bk'], 'L0_attn_Wv': _L0_attn_in['Wv'], 'L0_attn_bv': _L0_attn_in['bv'], 'L0_attn_Wo': _L0_attn_in['Wo'], 'L0_attn_bo': _L0_attn_in['bo'], 'L0_xattn_Wq': _L0_xattn_in['Wq'], 'L0_xattn_Wk': _L0_xattn_in['Wk'], 'L0_xattn_Wv': _L0_xattn_in['Wv'], 'L0_xattn_bv': _L0_xattn_in['bv'], 'L0_xattn_Wo': _L0_xattn_in['Wo'], 'L0_xattn_bo': _L0_xattn_in['bo'], 'L0_ffn_router_w1': _L0_ffn_in['router_w1'], 'L0_ffn_router_w2': _L0_ffn_in['router_w2'], 'L0_ffn_w1': _L0_ffn_in['w1'], 'L0_ffn_w2': _L0_ffn_in['w2'], 'L0_ffn_w3': _L0_ffn_in['w3']}

def reference(x, ctx_1024, L0_attn_Wq, L0_attn_bq, L0_attn_Wk, L0_attn_bk, L0_attn_Wv, L0_attn_bv, L0_attn_Wo, L0_attn_bo, L0_xattn_Wq, L0_xattn_Wk, L0_xattn_Wv, L0_xattn_bv, L0_xattn_Wo, L0_xattn_bo, L0_ffn_router_w1, L0_ffn_router_w2, L0_ffn_w1, L0_ffn_w2, L0_ffn_w3):
    import jax
    import jax.numpy as jnp

    def _L0_attn_ref(x, Wq, bq, Wk, bk, Wv, bv, Wo, bo):
        import jax, jax.numpy as jnp
        import numpy as np
        B, S, IN_DIM, D_MODEL, NUM_HEADS = (4, 256, 128, 128, 16)
        HEAD_DIM = D_MODEL // NUM_HEADS
        CAUSAL = True
        NEG = -9000000000000000.0

        def _xavier(key, shape):
            fan_out, fan_in = shape
            limit = (6.0 / (fan_in + fan_out)) ** 0.5
            return jax.random.uniform(key, shape, jnp.float32, -limit, limit)
        batch, seq, _ = x.shape
        q = x @ Wq.T + bq
        k = x @ Wk.T + bk
        v = x @ Wv.T + bv

        def split(t):
            return t.reshape(batch, seq, NUM_HEADS, HEAD_DIM).transpose(0, 2, 1, 3)
        q, k, v = (split(q), split(k), split(v))
        scores = jnp.einsum('bhqd,bhkd->bhqk', q, k) / jnp.sqrt(jnp.float32(HEAD_DIM))
        if CAUSAL:
            mask = jnp.tril(jnp.ones((seq, seq), bool))
            scores = jnp.where(mask, scores, jnp.float32(NEG))
        attn = jax.nn.softmax(scores, axis=-1)
        out = jnp.einsum('bhqk,bhkd->bhqd', attn, v)
        out = out.transpose(0, 2, 1, 3).reshape(batch, seq, D_MODEL)
        return out @ Wo.T + bo

    def _L0_xattn_ref(q, k, v, Wq, Wk, Wv, bv, Wo, bo):
        import jax, jax.numpy as jnp
        import numpy as np
        EMBED_PHI = 128
        EMBED_F = 128
        HIDDEN_F = 128
        N_HEADS = 16
        B, S = (2, 256)
        Bq, Sq, _ = q.shape
        hd = HIDDEN_F // N_HEADS
        scale = 1.0 / np.sqrt(hd)
        qh = (q @ Wq.T).reshape(Bq, Sq, N_HEADS, hd).transpose(0, 2, 1, 3)
        kh = (k @ Wk.T).reshape(Bq, Sq, N_HEADS, hd).transpose(0, 2, 1, 3)
        vh = (v @ Wv.T + bv).reshape(Bq, Sq, N_HEADS, hd).transpose(0, 2, 1, 3)
        scores = jnp.einsum('bhsd,bhtd->bhst', qh, kh) * scale
        mask = jnp.triu(jnp.ones((Sq, Sq), dtype=bool), k=0).at[0, 0].set(False)
        scores = jnp.where(mask, -jnp.inf, scores)
        probs = jax.nn.softmax(scores, axis=-1)
        out = jnp.einsum('bhst,bhtd->bhsd', probs, vh)
        out = out.transpose(0, 2, 1, 3).reshape(Bq, Sq, HIDDEN_F)
        return out @ Wo.T + bo

    def _L0_ffn_ref(hidden_states, router_w1, router_w2, w1, w2, w3):
        import jax, jax.numpy as jnp
        import numpy as np
        import math
        B, S, D = (4, 256, 128)
        E, DFF = (16, 256)
        CAP_FACTOR = 2.0
        ROUTER_HIDDEN = 128
        CAPACITY = int(math.ceil(S * CAP_FACTOR / E))
        b, s, d = hidden_states.shape
        e = w1.shape[0]
        cap = CAPACITY
        router_logits = jax.nn.silu(hidden_states @ router_w1) @ router_w2
        expert_probs = jax.nn.softmax(router_logits.transpose(0, 2, 1), axis=-1)
        expert_weights, token_indices = jax.lax.top_k(expert_probs, cap)
        expert_weights = expert_weights / (expert_weights.sum(-1, keepdims=True) + 1e-09)
        expert_inputs = jax.vmap(lambda h, i: h[i])(hidden_states, token_indices)
        gate = jax.nn.silu(jnp.einsum('becd,edf->becf', expert_inputs, w1))
        value = jnp.einsum('becd,edf->becf', expert_inputs, w2)
        expert_out = jnp.einsum('becf,efd->becd', gate * value, w3)
        weighted = expert_out * expert_weights[..., None]

        def combine(idx, vals):
            return jnp.zeros((s, d), vals.dtype).at[idx.reshape(-1)].add(vals.reshape(-1, d))
        output = jax.vmap(combine)(token_indices, weighted)
        return output
    x = x + _L0_attn_ref(_layernorm(x, axis=-1), L0_attn_Wq, L0_attn_bq, L0_attn_Wk, L0_attn_bk, L0_attn_Wv, L0_attn_bv, L0_attn_Wo, L0_attn_bo)
    x = x + _L0_xattn_ref(_layernorm(x, axis=-1), ctx_1024, ctx_1024, L0_xattn_Wq, L0_xattn_Wk, L0_xattn_Wv, L0_xattn_bv, L0_xattn_Wo, L0_xattn_bo)
    x = x + _L0_ffn_ref(_layernorm(x, axis=-1), L0_ffn_router_w1, L0_ffn_router_w2, L0_ffn_w1, L0_ffn_w2, L0_ffn_w3)
    return x

_drawn_inputs = setup_inputs


def setup_inputs(seed=0):
    import zlib

    import numpy as np

    out = dict(_drawn_inputs(seed))
    spreads = {'L0_attn_bq': (0.0, 0.445),
     'L0_attn_bk': (0.0, 0.8),
     'L0_attn_bv': (0.0, 0.1),
     'L0_attn_bo': (0.0, 0.1)}
    factors = {'L0_ffn_router_w1': 8.0,
     'L0_ffn_router_w2': 8.0,
     'L0_ffn_w1': 8.0,
     'L0_ffn_w2': 8.0,
     'L0_ffn_w3': 8.0}
    for name, (base, spread) in spreads.items():
        noise = np.random.default_rng([zlib.crc32(name.encode()), seed]).standard_normal(out[name].shape)
        drawn = base * np.exp(spread * noise) if base else spread * noise
        out[name] = jnp.asarray(drawn.astype(out[name].dtype))
    for name, factor in factors.items():
        out[name] = (out[name] * factor).astype(out[name].dtype)
    return out
```

```python
import numpy as np
import concourse.bass as bass
from concourse import mybir
from contextlib import ExitStack

B, S, D = 16, 128, 128
H, HD = 16, 8
E, CAP, F = 16, 32, 256
HT = 4
NG = B // HT
MT = F // 128
EPS = 1e-5
MASKED = -1e30
RSQRT_MAGIC = 1597463007
NEWTON = 3

C_ID, C_HM, C_IOTA = 0, 128, 128 + H
C_END = C_IOTA + CAP
WQ, WK, WV, WO, XQ, XK, XV, XO, RW1 = range(9)
BV, BO, XBV, XBO = range(4)


def constants():
    c = np.zeros((128, C_END), np.float32)
    c[:, C_ID:C_ID + 128] = np.eye(128)
    p = np.arange(128)
    c[:, C_HM:C_HM + H] = (p[:, None] // HD == np.arange(H)) * np.float32(HD ** -0.5)
    c[:, C_IOTA:C_IOTA + CAP] = np.arange(CAP)
    own = np.zeros((128, HT), np.float32)
    own[p, (p // HD) % HT] = 1.0
    q, k = p[:, None], p[None, :]
    causal = np.where(k <= q, 0.0, MASKED)
    strict = np.where((k < q) | ((q == 0) & (k == 0)), 0.0, MASKED)
    return np.concatenate([c, own], 1), np.stack([np.eye(128), causal, strict], 1).astype(np.float32)


class Stream:

    def __init__(self, name, sb, sem, keys_bd, probs):
        self.keys_bd = keys_bd
        self.probs = probs
        self.q = sb(f"{name}_q", [128, 128])
        self.v = sb(f"{name}_v", [128, 128])
        self.neg = [sb(f"{name}_neg{u}", [128, 8]) for u in range(2)]
        self.sums = [sb(f"{name}_sums{u}", [128, 8]) for u in range(2)]
        self.rec = [sb(f"{name}_rec{u}", [128, 8]) for u in range(2)]
        self.probs_t = [sb(f"{name}_pt{g}", [128, HT * 128]) for g in range(4)]
        self.heads = sb(f"{name}_heads", [128, HT, 128])
        self.keys_ready = sem(f"{name}_keys_ready")
        self.q_ready = sem(f"{name}_q_ready")
        self.v_ready = sem(f"{name}_v_ready")
        self.scored = sem(f"{name}_scored")
        self.maxed = sem(f"{name}_maxed")
        self.exped = sem(f"{name}_exped")
        self.rec_ready = sem(f"{name}_rec_ready")
        self.normed = sem(f"{name}_normed")
        self.turned = sem(f"{name}_turned")
        self.turn_copied = sem(f"{name}_turn_copied")
        self.mixed = sem(f"{name}_mixed")
        self.mix_copied = sem(f"{name}_mix_copied")
        self.projected = sem(f"{name}_projected")
        self.added = sem(f"{name}_added")


def decoder_kernel(nc, x, ctx_t, consts, masks, weights, bias_cols, bias_rows, rw2, w1, w2, w3, out):
    f32, bf16, i32 = mybir.dt.float32, mybir.dt.bfloat16, mybir.dt.int32
    ALU, ACT, AX = mybir.AluOpType, mybir.ActivationFunctionType, mybir.AxisListType
    ctx = ExitStack()
    with ctx:
        def sb(name, shape, dt=f32):
            return ctx.enter_context(nc.sbuf_tensor(name, shape, dt))

        def ps(name, shape):
            return ctx.enter_context(nc.psum_tensor(name, shape, f32))

        def sem(name):
            return ctx.enter_context(nc.semaphore(name))

        resid = sb("resid", [128, B, 128])
        kv = sb("kv", [128, 4 * B * 128])
        vx = sb("vx", [128, B, 128])
        qt = kv[:, 0:2048].rearrange("p (b q) -> p b q", b=B)
        kt = kv[:, 2048:4096].rearrange("p (b k) -> p b k", b=B)
        vs = kv[:, 4096:6144].rearrange("p (b k) -> p b k", b=B)
        kx = kv[:, 6144:8192].rearrange("p (b k) -> p b k", b=B)
        work = sb("work", [128, 8192])
        cst = sb("cst", [128, C_END + HT])
        maskf = sb("maskf", [128, 3, 128])
        ident = cst[:, C_ID:C_ID + 128]
        head_mask = cst[:, C_HM:C_HM + H]
        iota = cst[:, C_IOTA:C_IOTA + CAP]
        own = cst[:, C_END:C_END + HT]
        ident_b = sb("ident_b", [128, 128], bf16)
        mask_b = [sb(f"mask_b{i}", [128, HT, 128], bf16) for i in range(2)]
        wt = sb("wt", [128, 9, 128])
        wo_own = [sb(f"wo_own{i}", [128, HT, 128]) for i in range(2)]
        bcol = sb("bcol", [128, 2])
        brow = sb("brow", [128, 4, 128])
        rw2p = sb("rw2p", [128, 32])

        st_self = Stream("self", sb, sem, work[:, 0:2048].rearrange("p (h k) -> p h k", h=H),
                         [work[:, 4096 + 1024 * u:5120 + 1024 * u].rearrange("p (h k) -> p h k", h=8) for u in (0, 1)])
        st_cross = Stream("cross", sb, sem, work[:, 2048:4096].rearrange("p (h k) -> p h k", h=H),
                          [work[:, 6144 + 1024 * u:7168 + 1024 * u].rearrange("p (h k) -> p h k", h=8) for u in (0, 1)])

        bn6 = sb("bn6", [128, HT, 6])
        mv = sb("mv", [128, HT, 2])
        var = sb("var", [128, HT])
        rs = sb("rs", [128, HT])
        tmp = sb("tmp", [128, HT])
        rsi = sb("rsi", [128, HT], i32)
        normed4 = sb("normed4", [128, HT, 128])
        normed4_t = sb("normed4_t", [128, HT, 128])
        ctx4 = sb("ctx4", [128, HT, 128])
        after_self = sb("after_self", [128, 128])
        normed1 = sb("normed1", [128, 128])
        normed1_t = sb("normed1_t", [128, 128])

        hid = sb("hid", [128, HT, 128])
        hid_e = sb("hid_e", [128, HT, 128])
        lneg = sb("lneg", [128, 1])
        zsum = sb("zsum", [128, 1])
        probs_e = sb("probs_e", [128, 128])
        left = sb("left", [128, 128])
        top = sb("top", [128, CAP])
        tsum = sb("tsum", [128, 1])
        picked = sb("picked", [128, 128])
        place = sb("place", [128, 2, 128])
        ones = sb("ones", [128, 128])
        place_t = sb("place_t", [128, 2, 128])
        sel = [sb(f"sel{r}", [128, E, CAP]) for r in range(2)]
        selw = [sb(f"selw{r}", [128, E, CAP]) for r in range(2)]
        scatter = sb("scatter", [128, B, 4, 128])
        exp_in = kv[:, :].rearrange("p (e b c) -> p e b c", e=E, b=B)
        exp_out = work[:, :].rearrange("p (b m d) -> p b m d", b=B, m=4)
        exp_out_g = work[:, :].rearrange("p (g b m d) -> p g b m d", g=NG, b=HT, m=4)
        w1s = [sb(f"w1s{r}", [128, F]) for r in range(2)]
        w2s = [sb(f"w2s{r}", [128, F]) for r in range(2)]
        w3s = [sb(f"w3s{r}", [128, MT, 128]) for r in range(2)]
        gate_s = [sb(f"gate_s{m}", [128, 512]) for m in range(MT)]
        act_s = [sb(f"act_s{r}", [128, MT, 512]) for r in range(2)]
        y_s = [sb(f"y_s{r}", [128, NG, 128]) for r in range(2)]

        score_p = ps("score_p", [128, 4, HT, 128])
        turn_p = [ps(f"turn_p{i}", [128, HT, 128]) for i in range(2)]
        heads_p = ps("heads_p", [128, HT, 128])
        prep_p = ps("prep_p", [128, HT, 128])
        banks = [score_p[:, i] for i in range(4)] + [turn_p[0][:], turn_p[1][:], heads_p[:], prep_p[:]]

        s_x = sem("s_x")
        s_const = sem("s_const")
        s_ctx = sem("s_ctx")
        s_dve_const = sem("s_dve_const")
        s_pool_const = sem("s_pool_const")
        s_n4 = sem("s_n4")
        s_n4t = sem("s_n4t")
        s_n4c = sem("s_n4c")
        s_qp = sem("s_qp")
        s_kp = sem("s_kp")
        s_vp = sem("s_vp")
        s_kxp = sem("s_kxp")
        s_vxp = sem("s_vxp")
        s_qk_out = sem("s_qk_out")
        s_v_out = sem("s_v_out")
        s_h1 = sem("s_h1")
        s_h1t = sem("s_h1t")
        s_h1c = sem("s_h1c")
        s_xq = sem("s_xq")
        s_boc = sem("s_boc")
        s_r1 = sem("s_r1")
        s_r1e = sem("s_r1e")
        s_r1d = sem("s_r1d")
        s_r1s = sem("s_r1s")
        s_lg = sem("s_lg")
        s_lm = sem("s_lm")
        s_le = sem("s_le")
        s_place = sem("s_place")
        s_pt = sem("s_pt")
        s_pc = sem("s_pc")
        s_sel = sem("s_sel")
        s_selw = sem("s_selw")
        s_gat = sem("s_gat")
        s_gc = sem("s_gc")
        s_st = sem("s_st")
        s_sc = sem("s_sc")
        s_w = [sem(f"s_w{r}") for r in range(2)]
        s_gate = sem("s_gate")
        s_value = sem("s_value")
        s_silu = sem("s_silu")
        s_act = sem("s_act")
        s_y = sem("s_y")
        s_yc = sem("s_yc")
        s_yd = [sem(f"s_yd{r}") for r in range(2)]
        s_comb = sem("s_comb")
        s_fin = sem("s_fin")
        s_out = sem("s_out")

        CONSTS = 16 * 6

        block = ctx.enter_context(nc.Block())

        def steps(engine, step):
            step(0)
            step(1)
            with engine.Fori(2, B) as t:
                step(t)
            step(B)
            step(B + 1)

        class Plan:

            def __init__(self, t):
                inner = not isinstance(t, int)
                self.has_self = inner or t < B
                self.has_cross = inner or 1 <= t <= B
                self.mixes_cross = inner or t >= 2
                self.projects_self = inner or 1 <= t <= B
                self.before_self_scores = (st_cross, t - 2) if self.mixes_cross else None
                self.before_cross_scores = (st_self, t) if self.has_self else (st_cross, t - 2)
                self.before_cross_mix = (st_self, t - 1) if self.projects_self else (st_cross, t - 3)
                self.before_self_mix = ((st_cross, t - 2) if self.mixes_cross
                                        else (st_self, t - 1) if self.projects_self else None)

        @block.sync
        def _(sp):
            for g in range(NG):
                sp.dma_start(resid[:, HT * g:HT * g + HT, :],
                             x[HT * g:HT * g + HT].rearrange("b s d -> s b d")).then_inc(s_x, 16)
                if g == 0:
                    sp.dma_start(cst[:], consts).then_inc(s_const, 16)
                    sp.dma_start(wt[:], weights).then_inc(s_const, 16)
                    sp.dma_start(maskf[:], masks).then_inc(s_const, 16)
                    sp.dma_start(bcol[:], bias_cols).then_inc(s_const, 16)
                    sp.dma_start(brow[:], bias_rows).then_inc(s_const, 16)
            sp.wait_ge(s_pool_const, 1)
            sp.dma_start(rw2p[:, 0:E], rw2).then_inc(s_const, 16)
            sp.dma_start(ctx4[:], ctx_t[0]).then_inc(s_ctx, 16)
            with sp.Fori(1, NG) as g:
                sp.wait_ge(s_vxp, g)
                sp.wait_ge(s_kxp, g)
                sp.dma_start(ctx4[:], ctx_t[g]).then_inc(s_ctx, 16)

            def load(e, r):
                sp.dma_start(w1s[r][:], w1[e]).then_inc(s_w[r], 16)
                sp.dma_start(w2s[r][:], w2[e]).then_inc(s_w[r], 16)
                sp.dma_start(w3s[r][:], w3[e].rearrange("(m p) d -> p m d", m=MT)).then_inc(s_w[r], 16)

            def spread(m, e4):
                e = m * 4 + e4
                sp.wait_ge(s_yc, e + 1)
                for b4 in range(HT):
                    dst = exp_out_g[CAP * e4:CAP * e4 + CAP, :, b4, m, :]
                    sp.dma_start(dst, y_s[e4 % 2][CAP * b4:CAP * b4 + CAP, :, :]).then_inc(s_yd[e4 % 2], 16)

            load(0, 0)
            load(1, 1)
            with sp.Fori(0, E // 4 - 1) as m:
                for e4 in range(4):
                    spread(m, e4)
                    load(m * 4 + e4 + 2, e4 % 2)
            for e4 in range(4):
                spread(E // 4 - 1, e4)
                if e4 < 2:
                    load(E - 2 + e4, e4 % 2)
            for g in range(NG):
                sp.wait_ge(s_fin, HT * (g + 1))
                sp.dma_start(out[HT * g:HT * g + HT].rearrange("b s d -> s b d"),
                             resid[:, HT * g:HT * g + HT, :]).then_inc(s_out, 16)
            sp.wait_ge(s_out, 16 * NG)

        @block.tensor
        def _(pe):
            pe.wait_ge(s_const, CONSTS)
            with pe.Fori(0, NG) as g:
                pe.wait_ge(s_n4, g + 1)
                for b in range(HT):
                    last = nc.tensor.transpose(banks[0][:, b, :], normed4[:, b, :], ident)
                last.then_inc(s_n4t, 1)
                pe.wait_ge(s_ctx, 16 * g + 16)
                pe.wait_ge(s_qk_out, 3 * g)
                pe.wait_ge(s_v_out, 2 * g)
                nc.tensor.matmul(banks[4], wt[:, XK, :], ctx4[:], start=True, stop=True).then_inc(s_kxp, 1)
                for b in range(HT):
                    last = nc.tensor.matmul(banks[5][:, b, :], ctx4[:, b, :], wt[:, XV, :], start=True, stop=True)
                last.then_inc(s_vxp, 1)
                pe.wait_ge(s_n4c, g + 1)
                nc.tensor.matmul(banks[1], wt[:, WQ, :], normed4_t[:], start=True, stop=True).then_inc(s_qp, 1)
                nc.tensor.matmul(banks[2], wt[:, WK, :], normed4_t[:], start=True, stop=True).then_inc(s_kp, 1)
                for b in range(HT):
                    last = nc.tensor.matmul(banks[3][:, b, :], normed4_t[:, b, :], wt[:, WV, :], start=True, stop=True)
                last.then_inc(s_vp, 1)
            pe.wait_ge(s_qk_out, 3 * NG)
            pe.wait_ge(s_v_out, 2 * NG)
            pe.wait_ge(s_dve_const, 1)

            def score(st, n, u, before, mask):
                if before is not None:
                    pe.wait_ge(before[0].exped, before[1] * 2 + u + 1)
                if u == 0:
                    pe.wait_ge(st.keys_ready, n + 1)
                    pe.wait_ge(st.q_ready, n + 1)
                for i in (2 * u, 2 * u + 1):
                    nc.tensor.matmul(score_p[:, i], ident_b[:], mask[:], start=True, stop=False)
                    last = nc.tensor.matmul(score_p[:, i], st.q[:], st.keys_bd[:, HT * i:HT * i + HT, :],
                                            start=False, stop=True)
                last.then_inc(st.scored, 1)

            def mix(st, n, before, between=None):
                def values(g):
                    if g == 0:
                        pe.wait_ge(st.v_ready, n + 1)
                        if before is not None:
                            pe.wait_ge(before[0].added, before[1] + 1)
                    pe.wait_ge(st.turn_copied, n * 4 + g + 1)
                    rows = slice(32 * g, 32 * g + 32)
                    return nc.tensor.matmul(heads_p[rows], st.v[:, rows], st.probs_t[g][:], start=True, stop=True)

                for g in range(4):
                    if g % 2 == 0:
                        pe.wait_ge(st.normed, n * 2 + g // 2 + 1)
                    if g >= 2:
                        pe.wait_ge(st.turn_copied, n * 4 + g - 1)
                    elif before is not None:
                        pe.wait_ge(before[0].turn_copied, before[1] * 4 + g + 3)
                    for j in range(HT):
                        last = nc.tensor.transpose(turn_p[g % 2][:, j, :], st.probs[g // 2][:, HT * (g % 2) + j, :], ident)
                    last.then_inc(st.turned, 1)
                    if g >= 1:
                        values(g - 1)
                    if g == 2 and between is not None:
                        between()
                values(3).then_inc(st.mixed, 1)

            def project(st, n, i):
                pe.wait_ge(st.mix_copied, n + 1)
                for j in range(HT):
                    last = nc.tensor.matmul(heads_p[:, 0, :], st.heads[:, j, :], wo_own[i][:, j, :],
                                            start=(j == 0), stop=(j == HT - 1))
                last.then_inc(st.projected, 1)

            def step(t):
                plan = Plan(t)

                def turn_normed():
                    pe.wait_ge(s_h1, t)
                    if not isinstance(t, int) or t >= 2:
                        pe.wait_ge(st_cross.q_ready, t - 1)
                    nc.tensor.transpose(prep_p[:, 0, :], normed1[:], ident).then_inc(s_h1t, 1)

                if plan.has_self:
                    score(st_self, t, 0, plan.before_self_scores, mask_b[0])
                if plan.projects_self:
                    project(st_self, t - 1, 0)
                if plan.has_self:
                    score(st_self, t, 1, plan.before_self_scores, mask_b[0])
                if plan.mixes_cross:
                    mix(st_cross, t - 2, plan.before_cross_mix, turn_normed if plan.has_cross else None)
                elif plan.has_cross:
                    turn_normed()
                if plan.has_cross:
                    pe.wait_ge(s_h1c, t)
                    nc.tensor.matmul(prep_p[:, 1, :], wt[:, XQ, :], normed1_t[:], start=True, stop=True).then_inc(s_xq, 1)
                    score(st_cross, t - 1, 0, plan.before_cross_scores, mask_b[1])
                if plan.mixes_cross:
                    project(st_cross, t - 2, 1)
                if plan.has_cross:
                    score(st_cross, t - 1, 1, plan.before_cross_scores, mask_b[1])
                if plan.has_self:
                    mix(st_self, t, plan.before_self_mix)

            steps(pe, step)

            pe.wait_ge(st_cross.added, B)
            with pe.Fori(0, NG) as g:
                pe.wait_ge(s_n4, g + NG + 1)
                for b in range(HT):
                    last = nc.tensor.transpose(banks[0][:, b, :], normed4[:, b, :], ident)
                last.then_inc(s_n4t, 1)
                pe.wait_ge(s_n4c, g + NG + 1)
                nc.tensor.matmul(banks[1], wt[:, RW1, :], normed4_t[:], start=True, stop=True).then_inc(s_r1, 1)
                pe.wait_ge(s_r1s, g + 1)
                for b in range(HT):
                    last = nc.tensor.matmul(banks[2][32 * b:32 * b + 32, 0, :], rw2p[:], hid[:, b, :], start=True, stop=True)
                last.then_inc(s_lg, 1)
                pe.wait_ge(s_place, g + 1)
                for i in range(2):
                    last = nc.tensor.transpose(banks[3][:, i, :], place[:, i, :], ident)
                last.then_inc(s_pt, 1)
                for b in range(HT):
                    pe.wait_ge(s_sel, g * HT + b + 1)
                    if b < 2:
                        pe.wait_ge(s_gc, g * HT)
                        pe.wait_ge(s_sc, g * HT)
                    else:
                        pe.wait_ge(s_gc, g * HT + b - 1)
                        pe.wait_ge(s_sc, g * HT + b - 1)
                    nc.tensor.matmul(banks[4 + b % 2], normed4[:, b, :], sel[b % 2][:], start=True, stop=True).then_inc(s_gat, 1)
                    pe.wait_ge(s_selw, g * HT + b + 1)
                    for m in range(4):
                        last = nc.tensor.transpose(banks[6 + b % 2][:, m, :], selw[b % 2][:, 4 * m:4 * m + 4, :], ident)
                    last.then_inc(s_st, 1)

            def gate_value(e, e4):
                r = e4 % 2
                pe.wait_ge(s_w[r], (e - e4) * 24 + 48 * (e4 // 2 + 1))
                for m in range(MT):
                    if not (isinstance(e, int) and e == 0):
                        pe.wait_ge(s_act, e * MT + m - 1)
                    cols = slice(128 * m, 128 * m + 128)
                    nc.tensor.matmul(banks[m], w1s[r][:, cols], exp_in[:, e], start=True, stop=True).then_inc(s_gate, 1)
                    nc.tensor.matmul(banks[2 + m], w2s[r][:, cols], exp_in[:, e], start=True, stop=True).then_inc(s_value, 1)

            def outputs(e, e4):
                r = e4 % 2
                pe.wait_ge(s_act, e * MT + MT)
                if not (isinstance(e, int) and e < 2):
                    pe.wait_ge(s_yc, e - 1)
                for g in range(NG):
                    for m in range(MT):
                        last = nc.tensor.matmul(banks[4 + r][:, g, :], act_s[r][:, m, 128 * g:128 * g + 128],
                                                w3s[r][:, m, :], start=(m == 0), stop=(m == MT - 1))
                last.then_inc(s_y, 1)

            pe.wait_ge(s_gc, B)
            gate_value(0, 0)
            for e4 in range(3):
                gate_value(e4 + 1, e4 + 1)
                outputs(e4, e4)
            with pe.Fori(1, E // 4) as m4:
                for e4 in range(4):
                    gate_value(m4 * 4 + e4, e4)
                    outputs(m4 * 4 + e4 - 1, (e4 + 3) % 4)
            outputs(E - 1, 3)

            for r in range(2):
                pe.wait_ge(s_yd[r], 16 * HT * E // 2)
            pe.wait_ge(s_sc, B)
            pe.wait_ge(s_act, E * MT)
            for b in range(B):
                if b >= 4:
                    pe.wait_ge(s_fin, b - 3)
                for m in range(4):
                    last = nc.tensor.matmul(banks[b % 4][:, 0, :], scatter[:, b, m, :], exp_out[:, b, m, :],
                                            start=(m == 0), stop=(m == 3))
                last.then_inc(s_comb, 1)

        @block.scalar
        def _(act):
            act.wait_ge(s_const, CONSTS)
            with act.Fori(0, NG) as g:
                act.wait_ge(s_n4t, g + 1)
                if True:
                    act.wait_ge(s_vp, g)
                nc.scalar.copy(normed4_t[:], banks[0]).then_inc(s_n4c, 1)
                act.wait_ge(s_kxp, g + 1)
                nc.scalar.copy(kx[:, bass.ds(g * HT, HT), :], banks[4]).then_inc(s_qk_out, 1)
                act.wait_ge(s_qp, g + 1)
                nc.scalar.activation(qt[:, bass.ds(g * HT, HT), :], banks[1], ACT.Identity, bias=bcol[:, 0:1]).then_inc(s_qk_out, 1)
                act.wait_ge(s_kp, g + 1)
                nc.scalar.activation(kt[:, bass.ds(g * HT, HT), :], banks[2], ACT.Identity, bias=bcol[:, 1:2]).then_inc(s_qk_out, 1)
            act.wait_ge(s_v_out, 2 * NG)
            act.wait_ge(s_qk_out, 3 * NG)
            nc.scalar.copy(st_self.q[:], qt[:, 0, :]).then_inc(st_self.q_ready, 1)

            def exps(st, n, u):
                act.wait_ge(st.maxed, n * 2 + u + 1)
                if not (isinstance(n, int) and n == 0):
                    act.wait_ge(st.turned, n * 4 + 2 * u - 2)
                for h in range(8):
                    last = nc.scalar.activation(st.probs[u][:, h, :], score_p[:, 2 * u + h // HT, h % HT, :], ACT.Exp,
                                                bias=st.neg[u][:, h:h + 1], accum_out=st.sums[u][:, h:h + 1])
                last.then_inc(st.exped, 1)

            def step(t):
                plan = Plan(t)
                if plan.has_self:
                    exps(st_self, t, 0)
                    exps(st_self, t, 1)
                    if not (isinstance(t, int) and t == 0):
                        act.wait_ge(st_self.mixed, t)
                    nc.scalar.copy(st_self.v[:], vs[:, t, :]).then_inc(st_self.v_ready, 1)
                    if not isinstance(t, int) or t < B - 1:
                        act.wait_ge(st_self.scored, t * 2 + 2)
                        nc.scalar.copy(st_self.q[:], qt[:, t + 1, :]).then_inc(st_self.q_ready, 1)
                if plan.has_cross:
                    exps(st_cross, t - 1, 0)
                    exps(st_cross, t - 1, 1)
                    if plan.mixes_cross:
                        act.wait_ge(st_cross.mixed, t - 1)
                    nc.scalar.copy(st_cross.v[:], vx[:, t - 1, :]).then_inc(st_cross.v_ready, 1)

            step(0)
            step(1)
            with act.Fori(2, B - 1) as t:
                step(t)
            step(B - 1)
            step(B)
            step(B + 1)

            with act.Fori(0, NG) as g:
                act.wait_ge(s_n4t, g + NG + 1)
                nc.scalar.copy(normed4_t[:], banks[0]).then_inc(s_n4c, 1)
                act.wait_ge(s_r1, g + 1)
                nc.scalar.activation(hid_e[:], banks[1], ACT.Exp, scale=-1.0).then_inc(s_r1e, 1)
                act.wait_ge(s_lm, g + 1)
                nc.scalar.activation(probs_e[:], banks[2][:, 0, :], ACT.Exp, bias=lneg[:], accum_out=zsum[:]).then_inc(s_le, 1)
                act.wait_ge(s_pt, g + 1)
                nc.scalar.copy(place_t[:], banks[3][:, 0:2, :]).then_inc(s_pc, 1)
                for b in range(HT):
                    act.wait_ge(s_gat, g * HT + b + 1)
                    nc.scalar.copy(exp_in[:, :, g * HT + b, :],
                                   banks[4 + b % 2].rearrange("p a b -> p (a b)").rearrange("p (e c) -> p e c", e=E)
                                   ).then_inc(s_gc, 1)

            def silu(e):
                for m in range(MT):
                    act.wait_ge(s_gate, e * MT + m + 1)
                    if not (isinstance(e, int) and e == 0):
                        act.wait_ge(s_act, e * MT + m - 1)
                    nc.scalar.activation(gate_s[m][:], banks[m], ACT.Silu).then_inc(s_silu, 1)

            def copy_out(e, e4):
                act.wait_ge(s_y, e + 1)
                if not (isinstance(e, int) and e < 2):
                    act.wait_ge(s_yd[e4 % 2], (e - e4) * 8 * HT + 16 * HT * (e4 // 2))
                nc.scalar.copy(y_s[e4 % 2][:], banks[4 + e4 % 2]).then_inc(s_yc, 1)

            silu(0)
            for e4 in range(3):
                silu(e4 + 1)
                copy_out(e4, e4)
            with act.Fori(1, E // 4) as m4:
                for e4 in range(4):
                    silu(m4 * 4 + e4)
                    if e4 == 0:
                        act.wait_ge(s_y, m4 * 4)
                        act.wait_ge(s_yd[1], m4 * 32 * HT - 16 * HT)
                        nc.scalar.copy(y_s[1][:], banks[5]).then_inc(s_yc, 1)
                    else:
                        copy_out(m4 * 4 + e4 - 1, e4 - 1)
            copy_out(E - 1, 3)

        @block.gpsimd
        def _(pool):
            nc.gpsimd.memset(rw2p[:], 0.0).then_inc(s_pool_const, 1)
            nc.gpsimd.memset(ones[:], 1.0).then_inc(s_pool_const, 1)
            pool.wait_ge(s_qk_out, 3 * NG)

            def keys(st, src, n):
                if not (isinstance(n, int) and n == 0):
                    pool.wait_ge(st.scored, n * 2)
                nc.gpsimd.tensor_tensor(st.keys_bd, src[:, n, :].unsqueeze(1).broadcast_to([128, H, 128]),
                                        head_mask.unsqueeze(2).broadcast_to([128, H, 128]), ALU.mult
                                        ).then_inc(st.keys_ready, 1)

            def normalise(st, n):
                for u in range(2):
                    pool.wait_ge(st.rec_ready, n * 2 + u + 1)
                    nc.gpsimd.tensor_tensor(st.probs[u], st.probs[u], st.rec[u][:].unsqueeze(2).broadcast_to([128, 8, 128]),
                                            ALU.mult).then_inc(st.normed, 1)

            keys(st_self, kt, 0)
            keys(st_cross, kx, 0)

            def step(t):
                plan = Plan(t)
                if plan.has_self:
                    normalise(st_self, t)
                    if not isinstance(t, int) or t < B - 1:
                        keys(st_self, kt, t + 1)
                if plan.has_cross:
                    normalise(st_cross, t - 1)
                    if not isinstance(t, int) or t < B:
                        keys(st_cross, kx, t)

            step(0)
            step(1)
            with pool.Fori(2, B - 1) as t:
                step(t)
            step(B - 1)
            step(B)

            with pool.Fori(0, NG) as g:
                for b in range(HT):
                    pool.wait_ge(s_sel, g * HT + b + 1)
                    if b >= 2:
                        pool.wait_ge(s_st, g * HT + b - 1)
                    else:
                        pool.wait_ge(s_st, g * HT)
                    nc.gpsimd.tensor_tensor(selw[b % 2][:], sel[b % 2][:],
                                            place_t[:, 1, 32 * b:32 * b + E].unsqueeze(2).broadcast_to([128, E, CAP]),
                                            ALU.mult).then_inc(s_selw, 1)

        @block.vector
        def _(dve):
            def norm_chain(sources):
                k = len(sources)
                for i, source in enumerate(sources):
                    nc.vector.bn_stats(bn6[:, i, :], source)
                dve.drain()
                for i in range(k):
                    nc.vector.bn_aggr(mv[:, i, :], bn6[:, i, :])
                v, y, w = var[:, 0:k], rs[:, 0:k], tmp[:, 0:k]
                dve.drain()
                nc.vector.tensor_scalar(v, mv[:, 0:k, 1], EPS, None, ALU.add)
                dve.drain()
                nc.vector.tensor_scalar(rsi[:, 0:k], v.bitcast(i32), 1, None, ALU.logical_shift_right)
                dve.drain()
                nc.vector.tensor_scalar(y.bitcast(i32), rsi[:, 0:k], -1.0, float(RSQRT_MAGIC), ALU.mult, ALU.add)
                for _ in range(NEWTON):
                    dve.drain()
                    nc.vector.tensor_tensor(w, y, y, ALU.mult)
                    dve.drain()
                    nc.vector.scalar_tensor_tensor(w, w, -0.5, v, ALU.mult, ALU.mult)
                    dve.drain()
                    nc.vector.scalar_tensor_tensor(y, w, 1.5, y, ALU.add, ALU.mult)
                dve.drain()

            def normalise4(g, done):
                norm_chain([resid[:, g * HT + b, :] for b in range(HT)])
                dve.wait_ge(s_n4t, done)
                for b in range(HT):
                    last = nc.vector.tensor_scalar(normed4[:, b, :], resid[:, g * HT + b, :], mv[:, b, 0:1], rs[:, b:b + 1],
                                                   ALU.subtract, ALU.mult)
                last.then_inc(s_n4, 1)

            dve.wait_ge(s_const, CONSTS)
            with dve.Fori(0, NG) as g:
                dve.wait_ge(s_x, g * 16 + 16)
                normalise4(g, g)
                dve.drain()
                nc.vector.tensor_tensor(resid[:, bass.ds(g * HT, HT), :], resid[:, bass.ds(g * HT, HT), :],
                                        brow[:, BO, :].unsqueeze(1).broadcast_to([128, HT, 128]), ALU.add).then_inc(s_boc, 1)
                dve.wait_ge(s_vxp, g + 1)
                nc.vector.tensor_tensor(vx[:, bass.ds(g * HT, HT), :], banks[5],
                                        brow[:, XBV, :].unsqueeze(1).broadcast_to([128, HT, 128]), ALU.add).then_inc(s_v_out, 1)
                dve.wait_ge(s_vp, g + 1)
                nc.vector.tensor_tensor(vs[:, bass.ds(g * HT, HT), :], banks[3],
                                        brow[:, BV, :].unsqueeze(1).broadcast_to([128, HT, 128]), ALU.add).then_inc(s_v_out, 1)
            nc.vector.tensor_copy(ident_b[:], maskf[:, 0, :])
            for i in range(2):
                nc.vector.tensor_copy(mask_b[i][:], maskf[:, 1 + i, :].unsqueeze(1).broadcast_to([128, HT, 128]))
            for i, w in enumerate((WO, XO)):
                last = nc.vector.tensor_tensor(wo_own[i][:], wt[:, w, :].unsqueeze(1).broadcast_to([128, HT, 128]),
                                               own.unsqueeze(2).broadcast_to([128, HT, 128]), ALU.mult)
            last.then_inc(s_dve_const, 1)
            dve.wait_ge(s_boc, NG)

            def maximum(st, n, u):
                dve.wait_ge(st.scored, n * 2 + u + 1)
                nc.vector.tensor_reduce(st.neg[u][:], score_p[:, 2 * u:2 * u + 2].rearrange("p a h k -> p (a h) k"),
                                        AX.X, ALU.max, negate=True).then_inc(st.maxed, 1)

            def reciprocal(st, n, u):
                dve.wait_ge(st.exped, n * 2 + u + 1)
                nc.vector.reciprocal(st.rec[u][:], st.sums[u][:]).then_inc(st.rec_ready, 1)

            def copy_turned(st, n, g):
                dve.wait_ge(st.turned, n * 4 + g + 1)
                nc.vector.tensor_copy(st.probs_t[g][:], turn_p[g % 2][:]).then_inc(st.turn_copied, 1)

            def copy_heads(st, n):
                dve.wait_ge(st.mixed, n + 1)
                nc.vector.tensor_copy(st.heads[:], heads_p[:]).then_inc(st.mix_copied, 1)

            def step(t):
                plan = Plan(t)
                if plan.has_self:
                    maximum(st_self, t, 0)
                if plan.projects_self:
                    dve.wait_ge(st_self.projected, t)
                    nc.vector.tensor_tensor(after_self[:], heads_p[:, 0, :], resid[:, t - 1, :], ALU.add).then_inc(st_self.added, 1)
                    dve.wait_ge(st_self.added, t)
                    nc.vector.tensor_tensor(resid[:, t - 1, :], after_self[:], brow[:, XBO, :], ALU.add).then_inc(s_boc, 1)
                    norm_chain([after_self[:]])
                    nc.vector.tensor_scalar(normed1[:], after_self[:], mv[:, 0, 0:1], rs[:, 0:1],
                                            ALU.subtract, ALU.mult).then_inc(s_h1, 1)
                if plan.has_self:
                    maximum(st_self, t, 1)
                if plan.mixes_cross:
                    copy_turned(st_cross, t - 2, 0)
                    copy_turned(st_cross, t - 2, 1)
                if plan.has_self:
                    reciprocal(st_self, t, 0)
                if plan.mixes_cross:
                    copy_turned(st_cross, t - 2, 2)
                if plan.has_cross:
                    dve.wait_ge(s_h1t, t)
                    nc.vector.tensor_copy(normed1_t[:], prep_p[:, 0, :]).then_inc(s_h1c, 1)
                if plan.mixes_cross:
                    copy_turned(st_cross, t - 2, 3)
                if plan.has_cross:
                    dve.wait_ge(s_xq, t)
                    nc.vector.tensor_copy(st_cross.q[:], prep_p[:, 1, :]).then_inc(st_cross.q_ready, 1)
                if plan.has_self:
                    reciprocal(st_self, t, 1)
                if plan.mixes_cross:
                    copy_heads(st_cross, t - 2)
                if plan.has_cross:
                    maximum(st_cross, t - 1, 0)
                if plan.mixes_cross:
                    dve.wait_ge(st_cross.projected, t - 1)
                    nc.vector.tensor_tensor(resid[:, t - 2, :], heads_p[:, 0, :], resid[:, t - 2, :], ALU.add).then_inc(st_cross.added, 1)
                if plan.has_cross:
                    maximum(st_cross, t - 1, 1)
                if plan.has_self:
                    copy_turned(st_self, t, 0)
                    copy_turned(st_self, t, 1)
                if plan.has_cross:
                    reciprocal(st_cross, t - 1, 0)
                if plan.has_self:
                    copy_turned(st_self, t, 2)
                    copy_turned(st_self, t, 3)
                if plan.has_cross:
                    reciprocal(st_cross, t - 1, 1)
                if plan.has_self:
                    copy_heads(st_self, t)

            steps(dve, step)

            dve.wait_ge(st_cross.added, B)
            dve.wait_ge(s_pool_const, 2)
            with dve.Fori(0, NG) as g:
                dve.wait_ge(s_gat, g * HT)
                normalise4(g, g + NG)
                dve.wait_ge(s_r1e, g + 1)
                nc.vector.tensor_scalar(hid_e[:], hid_e[:], 1.0, None, ALU.add).then_inc(s_r1d, 1)
                dve.wait_ge(s_r1d, g * 2 + 1)
                nc.vector.reciprocal(hid_e[:], hid_e[:]).then_inc(s_r1d, 1)
                dve.wait_ge(s_r1d, g * 2 + 2)
                nc.vector.tensor_tensor(hid[:], hid_e[:], banks[1], ALU.mult).then_inc(s_r1s, 1)
                dve.wait_ge(s_lg, g + 1)
                nc.vector.tensor_reduce(lneg[:], banks[2][:, 0, :], AX.X, ALU.max, negate=True).then_inc(s_lm, 1)
                dve.wait_ge(s_le, g + 1)

                nc.vector.tensor_copy(left[:], probs_e[:])
                for i in range(CAP // 8):
                    dve.drain()
                    nc.vector.max(top[:, 8 * i:8 * i + 8], left[:])
                    dve.drain()
                    nc.vector.match_replace(left[:], top[:, 8 * i:8 * i + 8], left[:], -1.0)
                dve.drain()
                nc.vector.tensor_scalar(picked[:], left[:], 0.0, None, ALU.is_lt)
                nc.vector.reduce_sum(tsum[:], top[:], AX.X)
                dve.drain()
                nc.vector.tensor_tensor_scan(left[:], ones[:], picked[:], 0.0, ALU.mult, ALU.add)
                nc.vector.scalar_tensor_tensor(tsum[:], zsum[:], 1e-9, tsum[:], ALU.mult, ALU.add)
                dve.drain()
                nc.vector.tensor_tensor(place[:, 0, :], left[:], picked[:], ALU.mult)
                nc.vector.reciprocal(tsum[:], tsum[:])
                dve.drain()
                nc.vector.tensor_scalar(place[:, 0, :], place[:, 0, :], -1.0, None, ALU.add)
                nc.vector.scalar_tensor_tensor(place[:, 1, :], probs_e[:], tsum[:, 0:1], picked[:], ALU.mult, ALU.mult).then_inc(s_place, 1)
                dve.wait_ge(s_pc, g + 1)

                def select(b):
                    if b >= 2:
                        dve.wait_ge(s_selw, g * HT + b - 1)
                        dve.wait_ge(s_gat, g * HT + b - 1)
                    else:
                        dve.wait_ge(s_selw, g * HT)
                        dve.wait_ge(s_gat, g * HT)
                    nc.vector.tensor_tensor(sel[b % 2][:], place_t[:, 0, 32 * b:32 * b + E].unsqueeze(2).broadcast_to([128, E, CAP]),
                                            iota.unsqueeze(1).broadcast_to([128, E, CAP]), ALU.is_equal).then_inc(s_sel, 1)

                def copy_scatter(b):
                    dve.wait_ge(s_st, g * HT + b + 1)
                    nc.vector.tensor_copy(scatter[:, g * HT + b, :, :], banks[6 + b % 2]).then_inc(s_sc, 1)

                select(0)
                select(1)
                copy_scatter(0)
                select(2)
                copy_scatter(1)
                select(3)
                copy_scatter(2)
                copy_scatter(3)

            def activate(e, r):
                for m in range(MT):
                    dve.wait_ge(s_silu, e * MT + m + 1)
                    dve.wait_ge(s_value, e * MT + m + 1)
                    if not (isinstance(e, int) and e < 2):
                        dve.wait_ge(s_y, e - 1)
                    nc.vector.tensor_tensor(act_s[r][:, m, :], gate_s[m][:], banks[2 + m].rearrange("p a b -> p (a b)"),
                                            ALU.mult).then_inc(s_act, 1)

            activate(0, 0)
            activate(1, 1)
            with dve.Fori(1, E // 2) as e2:
                for r in range(2):
                    activate(e2 * 2 + r, r)

            for b in range(B):
                dve.wait_ge(s_comb, b + 1)
                nc.vector.tensor_tensor(resid[:, b, :], banks[b % 4][:, 0, :], resid[:, b, :], ALU.add).then_inc(s_fin, 1)


def kernel(x, ctx_1024, L0_attn_Wq, L0_attn_bq, L0_attn_Wk, L0_attn_bk, L0_attn_Wv, L0_attn_bv, L0_attn_Wo, L0_attn_bo,
           L0_xattn_Wq, L0_xattn_Wk, L0_xattn_Wv, L0_xattn_bv, L0_xattn_Wo, L0_xattn_bo,
           L0_ffn_router_w1, L0_ffn_router_w2, L0_ffn_w1, L0_ffn_w2, L0_ffn_w3):
    import concourse.bacc as bacc
    from concourse.bass_utils import run_bass_kernel_spmd

    consts, masks = constants()
    square = [L0_attn_Wq, L0_attn_Wk, L0_attn_Wv, L0_attn_Wo, L0_xattn_Wq, L0_xattn_Wk, L0_xattn_Wv, L0_xattn_Wo]
    weights = np.stack([np.asarray(w).T for w in square] + [np.asarray(L0_ffn_router_w1)], 1)
    rows = np.stack([np.asarray(r) for r in (L0_attn_bv, L0_attn_bo, L0_xattn_bv, L0_xattn_bo)])
    arrays = {
        "x": np.asarray(x),
        "ctx_t": np.asarray(ctx_1024).reshape(NG, HT * S, D).transpose(0, 2, 1),
        "consts": consts,
        "masks": masks,
        "weights": weights,
        "bias_cols": np.stack([np.asarray(L0_attn_bq), np.asarray(L0_attn_bk)], 1),
        "bias_rows": np.broadcast_to(rows, (128, 4, 128)),
        "rw2": np.asarray(L0_ffn_router_w2),
        "w1": np.asarray(L0_ffn_w1),
        "w2": np.asarray(L0_ffn_w2),
        "w3": np.asarray(L0_ffn_w3),
    }
    arrays = {k: np.ascontiguousarray(v) for k, v in arrays.items()}
    nc = bacc.Bacc("TRN2", target_bir_lowering=False, num_devices=1)
    aps = {k: nc.dram_tensor(k, v.shape, mybir.dt.from_np(v.dtype), kind="ExternalInput").ap() for k, v in arrays.items()}
    out = nc.dram_tensor("out", (B, S, D), mybir.dt.float32, kind="ExternalOutput").ap()
    decoder_kernel(nc, **aps, out=out)
    return run_bass_kernel_spmd(nc, [arrays], core_ids=[0]).results[0]["out"]
```

```python
import numpy as np
import concourse.bass as bass
from concourse import mybir
from contextlib import ExitStack

B, S, D = 16, 128, 128
H, HD = 16, 8
E, CAP, F = 16, 32, 256
HT = 4
NG = B // HT
MT = F // 128
EPS = 1e-5
MASKED = -1e30
RSQRT_MAGIC = 1597463007
NEWTON = 3

C_ID, C_HM, C_IOTA = 0, 128, 128 + H
C_END = C_IOTA + CAP
WQ, WK, WV, WO, XQ, XK, XV, XO, RW1 = range(9)
BV, BO, XBV, XBO = range(4)


def constants():
    c = np.zeros((128, C_END), np.float32)
    c[:, C_ID:C_ID + 128] = np.eye(128)
    p = np.arange(128)
    c[:, C_HM:C_HM + H] = (p[:, None] // HD == np.arange(H)) * np.float32(HD ** -0.5)
    c[:, C_IOTA:C_IOTA + CAP] = np.arange(1, CAP + 1)
    own = np.zeros((128, HT), np.float32)
    own[p, (p // HD) % HT] = 1.0
    q, k = p[:, None], p[None, :]
    causal = np.where(k <= q, 0.0, MASKED)
    strict = np.where((k < q) | ((q == 0) & (k == 0)), 0.0, MASKED)
    return np.concatenate([c, own], 1), np.stack([np.eye(128), causal, strict], 1).astype(np.float32)


def decoder_kernel(nc, x, ctx_t, consts, masks, weights, bias_cols, bias_rows, rw2, expert_w, out):
    f32, bf16, i32 = mybir.dt.float32, mybir.dt.bfloat16, mybir.dt.int32
    ALU, ACT, AX = mybir.AluOpType, mybir.ActivationFunctionType, mybir.AxisListType
    ctx = ExitStack()
    with ctx:
        def sb(name, shape, dt=f32):
            return ctx.enter_context(nc.sbuf_tensor(name, shape, dt))

        def ps(name, shape):
            return ctx.enter_context(nc.psum_tensor(name, shape, f32))

        def sem(name):
            return ctx.enter_context(nc.semaphore(name))

        resid = sb("resid", [128, B, 128])
        kv = sb("kv", [128, 4 * B * 128])
        qt = kv[:, 0:2048].rearrange("p (b q) -> p b q", b=B)
        kt = kv[:, 2048:4096].rearrange("p (b k) -> p b k", b=B)
        vt = kv[:, 4096:6144].rearrange("p (b k) -> p b k", b=B)
        work = sb("work", [128, 8192])
        cst = sb("cst", [128, C_END + HT])
        maskf = sb("maskf", [128, 3, 128])
        ident = cst[:, C_ID:C_ID + 128]
        head_mask = cst[:, C_HM:C_HM + H]
        iota = cst[:, C_IOTA:C_IOTA + CAP]
        own = cst[:, C_END:C_END + HT]
        ident_b = sb("ident_b", [128, 128], bf16)
        mask_b = [sb(f"mask_b{i}", [128, HT, 128], bf16) for i in range(2)]
        wt = sb("wt", [128, 9, 128])
        wo_own = [sb(f"wo_own{i}", [128, HT, 128]) for i in range(2)]
        bcol = sb("bcol", [128, 2])
        brow = sb("brow", [128, 4, 128])
        rw2p = sb("rw2p", [128, 32])

        keys_bd = [work[:, 2048 * r:2048 * r + 2048].rearrange("p (h k) -> p h k", h=H) for r in range(2)]
        queries = [sb(f"queries{r}", [128, 128]) for r in range(2)]
        values = [sb(f"values{r}", [128, 128]) for r in range(2)]
        probs = [work[:, 4096 + 1024 * u:5120 + 1024 * u].rearrange("p (h k) -> p h k", h=8) for u in (0, 1)]
        probs_t = [work[:, 6144 + 512 * i:6656 + 512 * i] for i in range(4)]
        neg_max = [sb(f"neg_max{u}", [128, 8]) for u in range(2)]
        sums = [sb(f"sums{r}", [128, H]) for r in range(2)]
        rec_small = sb("rec_small", [128, H])
        rec = [sb(f"rec{r}", [128, HT, 4, 32]) for r in range(2)]
        rec_t = [sb(f"rec_t{r}", [128, HT, 128]) for r in range(2)]
        heads = [sb(f"heads{r}", [128, HT, 128]) for r in range(2)]

        bn6 = sb("bn6", [128, B, 6])
        mv = sb("mv", [128, B, 2])
        var = sb("var", [128, B])
        rs = sb("rs", [128, B])
        tmp = sb("tmp", [128, B])
        rsi = sb("rsi", [128, B], i32)
        normed4 = sb("normed4", [128, HT, 128])
        normed4_t = sb("normed4_t", [128, HT, 128])
        ctx4 = sb("ctx4", [128, HT, 128])
        lneg = sb("lneg", [128, NG])
        zsum = sb("zsum", [128, NG])
        top = sb("top", [128, NG, CAP])
        tsum = sb("tsum", [128, NG])
        ones = sb("ones", [128, NG, 128])
        def by_group(area, i):
            return area[:, 512 * i:512 * i + 512].rearrange("p (g t) -> p g t", g=NG)
        norm_t = [by_group(kv, g) for g in range(NG)]
        hid = [by_group(kv, NG + g) for g in range(NG)]
        probs_e, left, picked = [by_group(kv, 2 * NG + i) for i in range(3)]
        norm = work[:, 0:2048].rearrange("p (b d) -> p b d", b=B)
        place = [by_group(work, 4 + i) for i in range(2)]
        place_t = [by_group(work, 6 + i) for i in range(2)]
        sel = [sb(f"sel{r}", [128, E, CAP]) for r in range(2)]
        selw = [sb(f"selw{r}", [128, E, CAP]) for r in range(2)]
        scatter = sb("scatter", [128, B, 4, 128])
        exp_in = kv[:, :].rearrange("p (e b c) -> p e b c", e=E, b=B)
        exp_out = work[:, :].rearrange("p (b m d) -> p b m d", b=B, m=4)
        exp_out_g = work[:, :].rearrange("p (g b m d) -> p g b m d", g=NG, b=HT, m=4)
        ws = [sb(f"ws{r}", [128, 3 * F]) for r in range(4)]
        w1s = [w[:, 0:F] for w in ws]
        w2s = [w[:, F:2 * F] for w in ws]
        w3s = [w[:, 2 * F:3 * F].rearrange("p (m d) -> p m d", m=MT) for w in ws]
        gate_s = [sb(f"gate_s{m}", [128, 512]) for m in range(MT)]
        act_s = [sb(f"act_s{r}", [128, MT, 512]) for r in range(2)]
        y_s = [sb(f"y_s{r}", [128, NG, 128]) for r in range(2)]

        score_p = ps("score_p", [128, 4, HT, 128])
        turn_p = [ps(f"turn_p{i}", [128, HT, 128]) for i in range(2)]
        heads_p = ps("heads_p", [128, HT, 128])
        aux_p = ps("aux_p", [128, HT, 128])
        banks = [score_p[:, i] for i in range(4)] + [turn_p[0][:], turn_p[1][:], heads_p[:], aux_p[:]]

        s_x = sem("s_x")
        s_const = sem("s_const")
        s_ctx = sem("s_ctx")
        s_dve_const = sem("s_dve_const")
        s_pool_const = sem("s_pool_const")
        s_n4 = sem("s_n4")
        s_n4t = sem("s_n4t")
        s_n4c = sem("s_n4c")
        s_qp = sem("s_qp")
        s_kp = sem("s_kp")
        s_vp = sem("s_vp")
        s_qk_out = sem("s_qk_out")
        s_v_out = sem("s_v_out")
        s_biased = sem("s_biased")
        s_keys = sem("s_keys")
        s_q = sem("s_q")
        s_v = sem("s_v")
        s_scored = sem("s_scored")
        s_maxed = sem("s_maxed")
        s_exped = sem("s_exped")
        s_rec = sem("s_rec")
        s_rec_turned = sem("s_rec_turned")
        s_rec_copied = sem("s_rec_copied")
        s_turned = sem("s_turned")
        s_turn_copied = sem("s_turn_copied")
        s_mixed = sem("s_mixed")
        s_heads = sem("s_heads")
        s_projected = sem("s_projected")
        s_added = sem("s_added")
        s_norm = sem("s_norm")
        s_norm_t = sem("s_norm_t")
        s_norm_tc = sem("s_norm_tc")
        s_hid = sem("s_hid")
        s_hid_s = sem("s_hid_s")
        s_logits = sem("s_logits")
        s_lmax = sem("s_lmax")
        s_lexp = sem("s_lexp")
        s_place = sem("s_place")
        s_place_t = sem("s_place_t")
        s_place_c = sem("s_place_c")
        s_sel = sem("s_sel")
        s_selw = sem("s_selw")
        s_gathered = sem("s_gathered")
        s_gat_copied = sem("s_gat_copied")
        s_scat = sem("s_scat")
        s_scat_copied = sem("s_scat_copied")
        s_w = [sem(f"s_w{r}") for r in range(4)]
        s_gate = sem("s_gate")
        s_value = sem("s_value")
        s_silu = sem("s_silu")
        s_act = sem("s_act")
        s_y = sem("s_y")
        s_yc = sem("s_yc")
        s_yd = [sem(f"s_yd{r}") for r in range(2)]
        s_comb = sem("s_comb")
        s_fin = sem("s_fin")
        s_out = sem("s_out")

        CONSTS = 16 * 6

        block = ctx.enter_context(nc.Block())

        JOBS = 2 * B
        PREPS = JOBS // HT

        def at_least(n, least):
            return not isinstance(n, int) or n >= least

        def steps(engine, step, slot):
            step(0)
            with engine.Fori(1, 3) as k:
                step(k, SELF)
            step(3)
            step(4)
            with engine.Fori(5, 7) as k:
                step(k, CROSS)
            step(7)
            slot(JOBS, 0, k=PREPS)
            slot(JOBS + 1, 1, k=PREPS)

        SELF, CROSS = 0, 1
        PIECES = {SELF: (0, 1, 2, 3), CROSS: (2, 0, 1, 3)}

        def kind_of(n, kind):
            return kind if not isinstance(n, int) else SELF if n < B else CROSS

        @block.sync
        def _(sp):
            for g in range(NG):
                sp.dma_start(resid[:, HT * g:HT * g + HT, :],
                             x[HT * g:HT * g + HT].rearrange("b s d -> s b d")).then_inc(s_x, 16)
                if g == 0:
                    sp.dma_start(cst[:], consts).then_inc(s_const, 16)
                    sp.dma_start(wt[:], weights).then_inc(s_const, 16)
                    sp.dma_start(maskf[:], masks).then_inc(s_const, 16)
                    sp.dma_start(bcol[:], bias_cols).then_inc(s_const, 16)
                    sp.dma_start(brow[:], bias_rows).then_inc(s_const, 16)
            sp.wait_ge(s_pool_const, 1)
            sp.dma_start(rw2p[:, 0:E], rw2).then_inc(s_const, 16)
            sp.dma_start(ctx4[:], ctx_t[0]).then_inc(s_ctx, 16)
            with sp.Fori(1, NG) as g:
                sp.wait_ge(s_vp, g + NG)
                sp.dma_start(ctx4[:], ctx_t[g]).then_inc(s_ctx, 16)

            def load(e, e4):
                sp.dma_start(ws[e4][:], expert_w[e]).then_inc(s_w[e4], 16)

            def spread(m, e4):
                sp.wait_ge(s_yc, m * 4 + e4 + 1)
                for b4 in range(HT):
                    dst = exp_out_g[CAP * e4:CAP * e4 + CAP, :, b4, m, :]
                    sp.dma_start(dst, y_s[e4 % 2][CAP * b4:CAP * b4 + CAP, :, :]).then_inc(s_yd[e4 % 2], 16)

            for e4 in range(4):
                load(e4, e4)
            with sp.Fori(0, E // 4 - 1) as m:
                for e4 in range(4):
                    sp.wait_ge(s_y, m * 4 + e4 + 1)
                    load(m * 4 + e4 + 4, e4)
                    spread(m, e4)
            for e4 in range(4):
                spread(E // 4 - 1, e4)
            for g in range(NG):
                sp.wait_ge(s_fin, HT * (g + 1))
                sp.dma_start(out[HT * g:HT * g + HT].rearrange("b s d -> s b d"),
                             resid[:, HT * g:HT * g + HT, :]).then_inc(s_out, 16)
            sp.wait_ge(s_out, 16 * NG)

        @block.tensor
        def _(pe):
            pe.wait_ge(s_const, CONSTS)

            def piece(q, i, kind, bank):
                wq, wk, wv = (WQ, WK, WV) if kind == SELF else (XQ, XK, XV)
                source = normed4_t if kind == SELF else ctx4
                if i == 0:
                    pe.wait_ge(s_n4, q + 1)
                    for b in range(HT):
                        last = nc.tensor.transpose(bank[:, b, :], normed4[:, b, :], ident)
                    last.then_inc(s_n4t, 1)
                elif i == 1:
                    pe.wait_ge(s_n4c, q + 1)
                    nc.tensor.matmul(bank, wt[:, wq, :], normed4_t[:], start=True, stop=True).then_inc(s_qp, 1)
                elif i == 2:
                    if kind == CROSS:
                        pe.wait_ge(s_ctx, q * 16 - 16 * (NG - 1))
                    nc.tensor.matmul(bank, wt[:, wk, :], source[:], start=True, stop=True).then_inc(s_kp, 1)
                else:
                    for b in range(HT):
                        last = nc.tensor.matmul(bank[:, b, :], source[:, b, :], wt[:, wv, :], start=True, stop=True)
                    last.then_inc(s_vp, 1)

            for i in range(4):
                piece(0, i, SELF, banks[i])
            pe.wait_ge(s_dve_const, 1)

            def score(n, r, u, kind):
                if at_least(n, 1):
                    pe.wait_ge(s_exped, n * 2 + u - 1)
                elif u == 0:
                    pe.wait_ge(s_qk_out, 2)
                    pe.wait_ge(s_v_out, 1)
                if u == 0:
                    pe.wait_ge(s_keys, n + 1)
                    pe.wait_ge(s_q, n + 1)
                for i in (2 * u, 2 * u + 1):
                    nc.tensor.matmul(score_p[:, i], ident_b[:], mask_b[kind][:], start=True, stop=False)
                    last = nc.tensor.matmul(score_p[:, i], queries[r][:], keys_bd[r][:, HT * i:HT * i + HT, :],
                                            start=False, stop=True)
                last.then_inc(s_scored, 1)

            def turn(n, g):
                if g % 2 == 0:
                    pe.wait_ge(s_exped, n * 2 + g // 2 + 1)
                if at_least(n, 1) or g >= 2:
                    pe.wait_ge(s_turn_copied, n * 4 + g - 1)
                for j in range(HT):
                    last = nc.tensor.transpose(turn_p[g % 2][:, j, :], probs[g // 2][:, HT * (g % 2) + j, :], ident)
                last.then_inc(s_turned, 1)

            def mix(n, r, g):
                if g == 0:
                    pe.wait_ge(s_v, n + 1)
                    if at_least(n, 1):
                        pe.wait_ge(s_added, n)
                pe.wait_ge(s_turn_copied, n * 4 + g + 1)
                rows = slice(32 * g, 32 * g + 32)
                last = nc.tensor.matmul(heads_p[rows], values[r][:, rows], probs_t[g], start=True, stop=True)
                if g == 3:
                    last.then_inc(s_mixed, 1)

            def turn_rec(n, r, i, q, nth=None):
                pe.wait_ge(s_rec, n + 1)
                if isinstance(n, int) and n >= HT * (PREPS - 1):
                    pe.wait_ge(s_rec_copied, n)
                    i = None
                if i == 0:
                    pe.wait_ge(s_n4c, q + 1)
                elif i == 3:
                    pe.wait_ge(s_v_out, q + 1)
                elif i is not None:
                    pe.wait_ge(s_qk_out, q * 2 + nth)
                for j in range(HT):
                    last = nc.tensor.transpose(aux_p[:, j, :], rec[r][:, j].rearrange("p g w -> p (g w)"), ident)
                last.then_inc(s_rec_turned, 1)

            def project(n, r, kind):
                pe.wait_ge(s_heads, n + 1)
                for j in range(HT):
                    last = nc.tensor.matmul(heads_p[:, 0, :], heads[r][:, j, :], wo_own[kind][:, j, :],
                                            start=(j == 0), stop=(j == HT - 1))
                last.then_inc(s_projected, 1)

            def slot(n, b, kind=None, prep=None, k=None):
                r = b % 2
                has, has1, has2 = not isinstance(n, int) or n < JOBS, at_least(n, 1) and (not isinstance(n, int) or n <= JOBS), at_least(n, 2)
                if has:
                    score(n, r, 0, kind_of(n, kind))
                if has2:
                    project(n - 2, r, kind_of(n - 2 if isinstance(n, int) else n, kind))
                if has1:
                    turn(n - 1, 0)
                    turn(n - 1, 1)
                    if b == 0 or prep is None:
                        turn_rec(n - 1, 1 - r, 3, k)
                    else:
                        done = PIECES[prep[1]][:b]
                        turn_rec(n - 1, 1 - r, done[-1], k + 1, sum(i in (1, 2) for i in done))
                if has:
                    score(n, r, 1, kind_of(n, kind))
                if has1:
                    mix(n - 1, 1 - r, 0)
                    mix(n - 1, 1 - r, 1)
                    turn(n - 1, 2)
                    turn(n - 1, 3)
                if prep is not None:
                    if has1:
                        pe.wait_ge(s_rec_copied, n)
                    piece(prep[0], PIECES[prep[1]][b], prep[1], aux_p[:])
                if has1:
                    mix(n - 1, 1 - r, 2)
                    mix(n - 1, 1 - r, 3)

            def step(k, kind=None):
                for b in range(HT):
                    n = k * HT + b
                    prep = None if isinstance(k, int) and k == PREPS - 1 else (k + 1, kind_of((k + 1) * HT if isinstance(k, int) else k, kind))
                    slot(n, b, kind, prep, k)

            steps(pe, step, slot)

            for g in range(NG):
                pe.wait_ge(s_norm, g + 1)
                if g == 0:
                    pe.wait_ge(s_added, JOBS)
                for b in range(HT):
                    last = nc.tensor.transpose(banks[g][:, b, :], norm[:, HT * g + b, :], ident)
                last.then_inc(s_norm_t, 1)
            for g in range(NG):
                pe.wait_ge(s_norm_tc, g + 1)
                nc.tensor.matmul(banks[4 + g], wt[:, RW1, :], norm_t[g], start=True, stop=True).then_inc(s_hid, 1)
            for g in range(NG):
                pe.wait_ge(s_hid_s, g + 1)
                for b in range(HT):
                    last = nc.tensor.matmul(banks[0][32 * b:32 * b + 32, g, :], rw2p[:], hid[g][:, b, :],
                                            start=True, stop=True)
                last.then_inc(s_logits, 1)
            for i in range(2):
                pe.wait_ge(s_place, i + 1)
                for g in range(NG):
                    last = nc.tensor.transpose(banks[1 + i][:, g, :], place[i][:, g, :], ident)
                last.then_inc(s_place_t, 1)
            for b in range(B):
                pe.wait_ge(s_sel, b + 1)
                if b >= 2:
                    pe.wait_ge(s_gat_copied, b - 1)
                nc.tensor.matmul(banks[4 + b % 2], norm[:, b, :], sel[b % 2][:], start=True, stop=True).then_inc(s_gathered, 1)
                pe.wait_ge(s_selw, b + 1)
                if b >= 2:
                    pe.wait_ge(s_scat_copied, b - 1)
                for m in range(4):
                    last = nc.tensor.transpose(banks[6 + b % 2][:, m, :], selw[b % 2][:, 4 * m:4 * m + 4, :], ident)
                last.then_inc(s_scat, 1)

            def gate_value(e, e4):
                pe.wait_ge(s_w[e4], (e - e4) * 4 + 16)
                for m in range(MT):
                    if not (isinstance(e, int) and e == 0):
                        pe.wait_ge(s_act, e * MT + m - 1)
                    cols = slice(128 * m, 128 * m + 128)
                    nc.tensor.matmul(banks[m], w1s[e4][:, cols], exp_in[:, e], start=True, stop=True).then_inc(s_gate, 1)
                    nc.tensor.matmul(banks[2 + m], w2s[e4][:, cols], exp_in[:, e], start=True, stop=True).then_inc(s_value, 1)

            def outputs(e, e4):
                r = e4 % 2
                pe.wait_ge(s_act, e * MT + MT)
                if not (isinstance(e, int) and e < 2):
                    pe.wait_ge(s_yc, e - 1)
                for g in range(NG):
                    for m in range(MT):
                        last = nc.tensor.matmul(banks[4 + r][:, g, :], act_s[r][:, m, 128 * g:128 * g + 128],
                                                w3s[e4][:, m, :], start=(m == 0), stop=(m == MT - 1))
                last.then_inc(s_y, 1)

            pe.wait_ge(s_gat_copied, B)
            gate_value(0, 0)
            for e4 in range(3):
                gate_value(e4 + 1, e4 + 1)
                outputs(e4, e4)
            with pe.Fori(1, E // 4) as m4:
                for e4 in range(4):
                    gate_value(m4 * 4 + e4, e4)
                    outputs(m4 * 4 + e4 - 1, (e4 + 3) % 4)
            outputs(E - 1, 3)

            for r in range(2):
                pe.wait_ge(s_yd[r], 16 * HT * E // 2)
            pe.wait_ge(s_scat_copied, B)
            pe.wait_ge(s_act, E * MT)
            for b in range(B):
                if b >= 4:
                    pe.wait_ge(s_fin, b - 3)
                for m in range(4):
                    last = nc.tensor.matmul(banks[b % 4][:, 0, :], scatter[:, b, m, :], exp_out[:, b, m, :],
                                            start=(m == 0), stop=(m == 3))
                last.then_inc(s_comb, 1)

        @block.scalar
        def _(act):
            act.wait_ge(s_const, CONSTS)

            def piece(q, i, kind, bank):
                group = (q if kind == SELF else q - NG) * HT
                if i == 0:
                    act.wait_ge(s_n4t, q + 1)
                    if at_least(q, 1):
                        act.wait_ge(s_qp, q)
                        act.wait_ge(s_vp, q)
                    nc.scalar.copy(normed4_t[:], bank).then_inc(s_n4c, 1)
                elif i in (1, 2):
                    act.wait_ge((s_qp, s_kp)[i - 1], q + 1)
                    out = (qt, kt)[i - 1][:, bass.ds(group, HT), :]
                    if kind == SELF:
                        last = nc.scalar.activation(out, bank, ACT.Identity, bias=bcol[:, i - 1:i])
                    else:
                        last = nc.scalar.copy(out, bank)
                    last.then_inc(s_qk_out, 1)

            for i in range(3):
                piece(0, i, SELF, banks[i])

            def exps(n, r, u):
                act.wait_ge(s_maxed, n * 2 + u + 1)
                if at_least(n, 1):
                    act.wait_ge(s_turned, n * 4 + 2 * u - 2)
                if at_least(n, 2) and u == 0:
                    act.wait_ge(s_rec, n - 1)
                for h in range(8):
                    last = nc.scalar.activation(probs[u][:, h, :], score_p[:, 2 * u + h // HT, h % HT, :], ACT.Exp,
                                                bias=neg_max[u][:, h:h + 1], accum_out=sums[r][:, 8 * u + h:8 * u + h + 1])
                last.then_inc(s_exped, 1)

            def slot(n, b, kind=None, prep=None, k=None):
                if not isinstance(n, int) or n < JOBS:
                    exps(n, b % 2, 0)
                if at_least(n, 1) and (not isinstance(n, int) or n <= JOBS):
                    act.wait_ge(s_rec_turned, n)
                    if at_least(n, 3):
                        act.wait_ge(s_heads, n - 2)
                    nc.scalar.copy(rec_t[1 - b % 2][:], aux_p[:]).then_inc(s_rec_copied, 1)
                if not isinstance(n, int) or n < JOBS:
                    exps(n, b % 2, 1)
                    if prep is not None and b < 3:
                        piece(prep[0], PIECES[prep[1]][b], prep[1], aux_p[:])

            def step(k, kind=None):
                for b in range(HT):
                    prep = None if isinstance(k, int) and k == PREPS - 1 else (k + 1, kind_of((k + 1) * HT if isinstance(k, int) else k, kind))
                    slot(k * HT + b, b, kind, prep, k)

            steps(act, step, slot)

            for g in range(NG):
                act.wait_ge(s_norm_t, g + 1)
                nc.scalar.copy(norm_t[g], banks[g]).then_inc(s_norm_tc, 1)
            for g in range(NG):
                act.wait_ge(s_hid, g + 1)
                nc.scalar.activation(hid[g], banks[4 + g], ACT.Silu).then_inc(s_hid_s, 1)
            for g in range(NG):
                if g == 0:
                    act.wait_ge(s_lmax, 1)
                nc.scalar.activation(probs_e[:, g, :], banks[0][:, g, :], ACT.Exp, bias=lneg[:, g:g + 1],
                                     accum_out=zsum[:, g:g + 1]).then_inc(s_lexp, 1)
            act.wait_ge(s_place_t, 2)
            nc.scalar.copy(place_t[1], banks[2]).then_inc(s_place_c, 1)
            with act.Fori(0, B // 2) as b2:
                for r in range(2):
                    act.wait_ge(s_gathered, b2 * 2 + r + 1)
                    nc.scalar.copy(exp_in[:, :, b2 * 2 + r, :],
                                   banks[4 + r].rearrange("p a b -> p (a b)").rearrange("p (e c) -> p e c", e=E)
                                   ).then_inc(s_gat_copied, 1)

            def silu(e):
                for m in range(MT):
                    act.wait_ge(s_gate, e * MT + m + 1)
                    if not (isinstance(e, int) and e == 0):
                        act.wait_ge(s_act, e * MT + m - 1)
                    nc.scalar.activation(gate_s[m][:], banks[m], ACT.Silu).then_inc(s_silu, 1)

            def copy_out(e, e4):
                act.wait_ge(s_y, e + 1)
                if not (isinstance(e, int) and e < 2):
                    act.wait_ge(s_yd[e4 % 2], (e - e4) * 8 * HT + 16 * HT * (e4 // 2))
                nc.scalar.copy(y_s[e4 % 2][:], banks[4 + e4 % 2]).then_inc(s_yc, 1)

            silu(0)
            for e4 in range(3):
                silu(e4 + 1)
                copy_out(e4, e4)
            with act.Fori(1, E // 4) as m4:
                for e4 in range(4):
                    silu(m4 * 4 + e4)
                    if e4 == 0:
                        act.wait_ge(s_y, m4 * 4)
                        act.wait_ge(s_yd[1], m4 * 32 * HT - 16 * HT)
                        nc.scalar.copy(y_s[1][:], banks[5]).then_inc(s_yc, 1)
                    else:
                        copy_out(m4 * 4 + e4 - 1, e4 - 1)
            copy_out(E - 1, 3)

        @block.gpsimd
        def _(pool):
            nc.gpsimd.memset(rw2p[:], 0.0).then_inc(s_pool_const, 1)
            nc.gpsimd.memset(ones[:, :, 1:128], 1.0)
            nc.gpsimd.memset(ones[:, :, 0:1], 0.0).then_inc(s_pool_const, 1)

            def add_bias(q, kind):
                pool.wait_ge(s_n4, q + 1)
                group = resid[:, bass.ds((q if kind == SELF else q - NG) * HT, HT), :]
                row = brow[:, BO if kind == SELF else XBO, :].unsqueeze(1).broadcast_to([128, HT, 128])
                nc.gpsimd.tensor_tensor(group, group, row, ALU.add).then_inc(s_biased, 1)

            def fetch(n, r, kind, q=None):
                batch = n if kind == SELF else n - B
                if q is not None:
                    pool.wait_ge(s_qk_out, q * 2 + 2)
                if at_least(n, 2):
                    pool.wait_ge(s_scored, n * 2 - 2)
                nc.gpsimd.tensor_tensor(keys_bd[r], kt[:, batch, :].unsqueeze(1).broadcast_to([128, H, 128]),
                                        head_mask.unsqueeze(2).broadcast_to([128, H, 128]), ALU.mult
                                        ).then_inc(s_keys, 1)
                nc.gpsimd.tensor_copy(queries[r][:], qt[:, batch, :]).then_inc(s_q, 1)

            def fetch_values(n, r, kind, q=None):
                if q is not None:
                    pool.wait_ge(s_v_out, q + 1)
                if at_least(n, 2):
                    pool.wait_ge(s_mixed, n - 1)
                nc.gpsimd.tensor_copy(values[r][:], vt[:, n if kind == SELF else n - B, :]).then_inc(s_v, 1)

            pool.wait_ge(s_const, CONSTS)
            fetch(0, 0, SELF, 0)
            add_bias(0, SELF)

            def step(k, kind=None):
                last_step = isinstance(k, int) and k == PREPS - 1
                for b in range(HT):
                    n = k * HT + b
                    fetch_values(n, b % 2, kind_of(n, kind), k if b == 0 else None)
                    if not (last_step and b == 3):
                        fetch(n + 1, (b + 1) % 2, kind_of(n + 1 if isinstance(n, int) else n, kind), k + 1 if b == 3 else None)
                    if b == 2 and not last_step:
                        add_bias(k + 1, kind_of((k + 1) * HT if isinstance(k, int) else k, kind))

            def no_slot(n, b, k):
                pass

            steps(pool, step, no_slot)

            pool.wait_ge(s_place_c, 1)
            for b in range(B):
                pool.wait_ge(s_sel, b + 1)
                if b >= 2:
                    pool.wait_ge(s_scat, b - 1)
                weight = place_t[1][:, b // HT, 32 * (b % HT):32 * (b % HT) + E]
                nc.gpsimd.tensor_tensor(selw[b % 2][:], sel[b % 2][:], weight.unsqueeze(2).broadcast_to([128, E, CAP]),
                                        ALU.mult).then_inc(s_selw, 1)

        @block.vector
        def _(dve):
            def stats(first, col):
                for i in range(HT):
                    nc.vector.bn_stats(bn6[:, col + i, :], resid[:, first + i, :])
                dve.drain()
                for i in range(HT):
                    nc.vector.bn_aggr(mv[:, col + i, :], bn6[:, col + i, :])

            def rsqrt(cols):
                v, y, w, i = var[:, cols], rs[:, cols], tmp[:, cols], rsi[:, cols]
                dve.drain()
                nc.vector.tensor_scalar(v, mv[:, cols, 1], EPS, None, ALU.add)
                dve.drain()
                nc.vector.tensor_scalar(i, v.bitcast(i32), 1, None, ALU.logical_shift_right)
                dve.drain()
                nc.vector.tensor_scalar(y.bitcast(i32), i, -1.0, float(RSQRT_MAGIC), ALU.mult, ALU.add)
                for _ in range(NEWTON):
                    dve.drain()
                    nc.vector.tensor_tensor(w, y, y, ALU.mult)
                    dve.drain()
                    nc.vector.scalar_tensor_tensor(w, w, -0.5, v, ALU.mult, ALU.mult)
                    dve.drain()
                    nc.vector.scalar_tensor_tensor(y, w, 1.5, y, ALU.add, ALU.mult)
                dve.drain()

            def normalise(first, col, target=None, count=0):
                if not (isinstance(count, int) and count == 0):
                    dve.wait_ge(s_n4t, count)
                for b in range(HT):
                    last = nc.vector.tensor_scalar((normed4 if target is None else target)[:, b, :], resid[:, first + b, :], mv[:, bass.ds(col + b, 1), 0],
                                                   rs[:, bass.ds(col + b, 1)], ALU.subtract, ALU.mult)
                return last

            dve.wait_ge(s_const, CONSTS)
            nc.vector.tensor_copy(ident_b[:], maskf[:, 0, :])
            for i in range(2):
                nc.vector.tensor_copy(mask_b[i][:], maskf[:, 1 + i, :].unsqueeze(1).broadcast_to([128, HT, 128]))
            for i, w in enumerate((WO, XO)):
                last = nc.vector.tensor_tensor(wo_own[i][:], wt[:, w, :].unsqueeze(1).broadcast_to([128, HT, 128]),
                                               own.unsqueeze(2).broadcast_to([128, HT, 128]), ALU.mult)
            last.then_inc(s_dve_const, 1)
            for g in range(NG):
                dve.wait_ge(s_x, g * 16 + 16)
                stats(g * HT, g * HT)
            rsqrt(slice(0, B))
            normalise(0, 0).then_inc(s_n4, 1)

            def values_out(q, kind, bank):
                dve.wait_ge(s_vp, q + 1)
                group = (q if kind == SELF else q - NG) * HT
                row = brow[:, BV if kind == SELF else XBV, :].unsqueeze(1).broadcast_to([128, HT, 128])
                return nc.vector.tensor_tensor(vt[:, bass.ds(group, HT), :], bank, row, ALU.add).then_inc(s_v_out, 1)

            values_out(0, SELF, banks[3])

            def maximum(n, u):
                dve.wait_ge(s_scored, n * 2 + u + 1)
                nc.vector.tensor_reduce(neg_max[u][:], score_p[:, 2 * u:2 * u + 2].rearrange("p a h k -> p (a h) k"),
                                        AX.X, ALU.max, negate=True).then_inc(s_maxed, 1)

            def copy_turned(n, g):
                dve.wait_ge(s_turned, n * 4 + g + 1)
                nc.vector.tensor_copy(probs_t[g], turn_p[g % 2][:].rearrange("p a b -> p (a b)")).then_inc(s_turn_copied, 1)

            def slot(n, b, kind=None, prep=None, k=None):
                r = b % 2
                has, has1, has2 = not isinstance(n, int) or n < JOBS, at_least(n, 1) and (not isinstance(n, int) or n <= JOBS), at_least(n, 2)
                if has:
                    maximum(n, 0)
                if has1:
                    dve.wait_ge(s_exped, n * 2)
                    nc.vector.reciprocal(rec_small[:], sums[1 - r][:])
                    dve.drain()
                    if at_least(n, 3):
                        dve.wait_ge(s_rec_turned, n - 2)
                    nc.vector.tensor_copy(rec[1 - r][:], rec_small[:].rearrange("p (g j) -> p j g", j=HT).unsqueeze(3)
                                          .broadcast_to([128, HT, 4, 32])).then_inc(s_rec, 1)
                if has2:
                    batch = n - 2 if kind_of(n - 2 if isinstance(n, int) else n, kind) == SELF else n - 2 - B
                    if b == 2:
                        dve.wait_ge(s_biased, k + 1)
                    dve.wait_ge(s_projected, n - 1)
                    nc.vector.tensor_tensor(resid[:, batch, :], heads_p[:, 0, :], resid[:, batch, :], ALU.add).then_inc(s_added, 1)
                if has1:
                    copy_turned(n - 1, 0)
                    copy_turned(n - 1, 1)
                if has:
                    maximum(n, 1)
                if has1:
                    copy_turned(n - 1, 2)
                    copy_turned(n - 1, 3)
                if prep is not None and b == 0 and prep[1] == SELF:
                    normalise(prep[0] * HT, prep[0] * HT, count=prep[0]).then_inc(s_n4, 1)
                if prep is not None and b == 3:
                    values_out(prep[0], prep[1], aux_p[:])
                if has1:
                    dve.wait_ge(s_rec_copied, n)
                    dve.wait_ge(s_mixed, n)
                    nc.vector.tensor_tensor(heads[1 - r][:], heads_p[:], rec_t[1 - r][:], ALU.mult).then_inc(s_heads, 1)
                if prep is not None and b == 0 and prep[1] == CROSS:
                    dve.drain()
                    stats((prep[0] - NG) * HT, 0)
                    rsqrt(slice(0, HT))
                    normalise((prep[0] - NG) * HT, 0, count=prep[0]).then_inc(s_n4, 1)

            def step(k, kind=None):
                for b in range(HT):
                    prep = None if isinstance(k, int) and k == PREPS - 1 else (k + 1, kind_of((k + 1) * HT if isinstance(k, int) else k, kind))
                    slot(k * HT + b, b, kind, prep, k)

            steps(dve, step, slot)

            dve.wait_ge(s_added, JOBS)
            for g in range(NG):
                stats(g * HT, g * HT)
            rsqrt(slice(0, B))
            for g in range(NG):
                normalise(g * HT, g * HT, norm[:, HT * g:HT * g + HT]).then_inc(s_norm, 1)
            dve.wait_ge(s_logits, NG)
            nc.vector.tensor_reduce(lneg[:], banks[0], AX.X, ALU.max, negate=True).then_inc(s_lmax, 1)

            for i in range(CAP // 8):
                source = probs_e if i == 0 else left
                for g in range(NG):
                    if i == 0:
                        dve.wait_ge(s_lexp, g + 1)
                    nc.vector.max(top[:, g, 8 * i:8 * i + 8], source[:, g, :])
                dve.drain()
                for g in range(NG):
                    nc.vector.match_replace(left[:, g, :], top[:, g, 8 * i:8 * i + 8], source[:, g, :], -1.0)
                dve.drain()
            nc.vector.tensor_scalar(picked, left, 0.0, None, ALU.is_lt)
            nc.vector.reduce_sum(tsum[:], top[:], AX.X)
            dve.drain()
            dve.wait_ge(s_pool_const, 2)
            nc.vector.tensor_tensor_scan(left.rearrange("p g t -> p (g t)"), ones[:].rearrange("p g t -> p (g t)"),
                                         picked.rearrange("p g t -> p (g t)"), 0.0, ALU.mult, ALU.add)
            nc.vector.scalar_tensor_tensor(tsum[:], zsum[:], 1e-9, tsum[:], ALU.mult, ALU.add)
            dve.drain()
            nc.vector.tensor_tensor(place[0], left, picked, ALU.mult).then_inc(s_place, 1)
            nc.vector.reciprocal(tsum[:], tsum[:])
            dve.drain()
            for g in range(NG):
                last = nc.vector.scalar_tensor_tensor(place[1][:, g, :], probs_e[:, g, :], tsum[:, g:g + 1],
                                                      picked[:, g, :], ALU.mult, ALU.mult)
            last.then_inc(s_place, 1)
            dve.wait_ge(s_place_t, 1)
            nc.vector.tensor_copy(place_t[0], banks[1])
            dve.drain()

            def select(b):
                if b >= 2:
                    dve.wait_ge(s_selw, b - 1)
                    dve.wait_ge(s_gathered, b - 1)
                slots = place_t[0][:, b // HT, 32 * (b % HT):32 * (b % HT) + E]
                nc.vector.tensor_tensor(sel[b % 2][:], slots.unsqueeze(2).broadcast_to([128, E, CAP]),
                                        iota.unsqueeze(1).broadcast_to([128, E, CAP]), ALU.is_equal).then_inc(s_sel, 1)

            select(0)
            for b in range(B):
                if b < B - 1:
                    select(b + 1)
                dve.wait_ge(s_scat, b + 1)
                nc.vector.tensor_copy(scatter[:, b, :, :], banks[6 + b % 2]).then_inc(s_scat_copied, 1)

            def activate(e, r):
                for m in range(MT):
                    dve.wait_ge(s_silu, e * MT + m + 1)
                    dve.wait_ge(s_value, e * MT + m + 1)
                    if not (isinstance(e, int) and e < 2):
                        dve.wait_ge(s_y, e - 1)
                    nc.vector.tensor_tensor(act_s[r][:, m, :], gate_s[m][:], banks[2 + m].rearrange("p a b -> p (a b)"),
                                            ALU.mult).then_inc(s_act, 1)

            activate(0, 0)
            activate(1, 1)
            with dve.Fori(1, E // 2) as e2:
                for r in range(2):
                    activate(e2 * 2 + r, r)

            for b in range(B):
                dve.wait_ge(s_comb, b + 1)
                nc.vector.tensor_tensor(resid[:, b, :], banks[b % 4][:, 0, :], resid[:, b, :], ALU.add).then_inc(s_fin, 1)


def kernel(x, ctx_1024, L0_attn_Wq, L0_attn_bq, L0_attn_Wk, L0_attn_bk, L0_attn_Wv, L0_attn_bv, L0_attn_Wo, L0_attn_bo,
           L0_xattn_Wq, L0_xattn_Wk, L0_xattn_Wv, L0_xattn_bv, L0_xattn_Wo, L0_xattn_bo,
           L0_ffn_router_w1, L0_ffn_router_w2, L0_ffn_w1, L0_ffn_w2, L0_ffn_w3):
    import concourse.bacc as bacc
    from concourse.bass_utils import run_bass_kernel_spmd

    consts, masks = constants()
    square = [L0_attn_Wq, L0_attn_Wk, L0_attn_Wv, L0_attn_Wo, L0_xattn_Wq, L0_xattn_Wk, L0_xattn_Wv, L0_xattn_Wo]
    weights = np.stack([np.asarray(w).T for w in square] + [np.asarray(L0_ffn_router_w1)], 1)
    rows = np.stack([np.asarray(r) for r in (L0_attn_bv, L0_attn_bo, L0_xattn_bv, L0_xattn_bo)])
    w3 = np.asarray(L0_ffn_w3).reshape(E, MT, 128, D).transpose(0, 2, 1, 3).reshape(E, 128, MT * D)
    expert_w = np.concatenate([np.asarray(L0_ffn_w1), np.asarray(L0_ffn_w2), w3], 2)
    arrays = {
        "x": np.asarray(x),
        "ctx_t": np.asarray(ctx_1024).reshape(NG, HT * S, D).transpose(0, 2, 1),
        "consts": consts,
        "masks": masks,
        "weights": weights,
        "bias_cols": np.stack([np.asarray(L0_attn_bq), np.asarray(L0_attn_bk)], 1),
        "bias_rows": np.broadcast_to(rows, (128, 4, 128)),
        "rw2": np.asarray(L0_ffn_router_w2),
        "expert_w": expert_w,
    }
    arrays = {k: np.ascontiguousarray(v) for k, v in arrays.items()}
    nc = bacc.Bacc("TRN2", target_bir_lowering=False, num_devices=1)
    aps = {k: nc.dram_tensor(k, v.shape, mybir.dt.from_np(v.dtype), kind="ExternalInput").ap() for k, v in arrays.items()}
    out = nc.dram_tensor("out", (B, S, D), mybir.dt.float32, kind="ExternalOutput").ap()
    decoder_kernel(nc, **aps, out=out)
    return run_bass_kernel_spmd(nc, [arrays], core_ids=[0]).results[0]["out"]
```

```python
import numpy as np
import concourse.bass as bass
from concourse import mybir
from contextlib import ExitStack

B, S, D = 16, 128, 128
H, HD = 16, 8
E, CAP, F = 16, 32, 256
HT = 4
NG = B // HT
MT = F // 128
EPS = 1e-5
SCALE = HD ** -0.5
MASKED = -1e30
RSQRT_MAGIC = 1597463007
NEWTON = 3
LOW_BITS = 12

C_ID, C_IOTA = 0, 128
C_END = C_IOTA + CAP
WQ, WK, WV, WO, XQ, XK, XV, XO, RW1 = range(9)
BV, BO, XBV, XBO = range(4)


def constants():
    c = np.zeros((128, C_END), np.float32)
    c[:, C_ID:C_ID + 128] = np.eye(128)
    p = np.arange(128)
    c[:, C_IOTA:C_IOTA + CAP] = np.arange(1, CAP + 1)
    own = np.zeros((128, HT), np.float32)
    own[p, (p // HD) % HT] = 1.0
    q, k = p[:, None], p[None, :]
    causal = np.where(k <= q, 0.0, MASKED)
    strict = np.where((k < q) | ((q == 0) & (k == 0)), 0.0, MASKED)
    return np.concatenate([c, own], 1), np.stack([np.eye(128), causal, strict], 1).astype(np.float32)


def decoder_kernel(nc, x, ctx_t, consts, masks, weights, bias_cols, bias_rows, rw2, expert_w, scratch, out):
    f32, f32r, bf16, i32 = mybir.dt.float32, mybir.dt.float32r, mybir.dt.bfloat16, mybir.dt.int32
    ALU, ACT, AX = mybir.AluOpType, mybir.ActivationFunctionType, mybir.AxisListType
    ctx = ExitStack()
    with ctx:
        def sb(name, shape, dt=f32):
            return ctx.enter_context(nc.sbuf_tensor(name, shape, dt))

        def ps(name, shape):
            return ctx.enter_context(nc.psum_tensor(name, shape, f32))

        def sem(name):
            return ctx.enter_context(nc.semaphore(name))

        resid = sb("resid", [128, B, 128])
        kv = sb("kv", [128, 4 * B * 128])
        q_parts = kv[:, 0:1024].rearrange("p (s t) -> p s t", s=2)
        k_parts = kv[:, 1024:2048].rearrange("p (s t) -> p s t", s=2)
        ctx_all = kv[:, 2048:4096].rearrange("p (g t) -> p g t", g=NG)
        vt = kv[:, 4096:6144].rearrange("p (b k) -> p b k", b=B)
        late = sb("late", [128, B * 4 * 128])
        q_stack = [sb(f"q_stack{b}", [128, 4, 128]) for b in range(HT)]
        k_stack = late[:, 0:4096].rearrange("p (r g b t) -> p r g b t", r=2, g=4, b=HT)
        work = sb("work", [128, B * 4 * 128])
        cst = sb("cst", [128, C_END + HT])
        maskf = sb("maskf", [128, 3, 128])
        ident = cst[:, C_ID:C_ID + 128]
        iota = cst[:, C_IOTA:C_IOTA + CAP]
        own = cst[:, C_END:C_END + HT]
        ident_b = sb("ident_b", [128, 128], bf16)
        mask_b = [sb(f"mask_b{i}", [128, HT, 128], bf16) for i in range(2)]
        wt = sb("wt", [128, 9, 128])
        wo_own = [sb(f"wo_own{i}", [128, HT, 128]) for i in range(2)]
        bcol = sb("bcol", [128, 2])
        bq_scaled = sb("bq_scaled", [128, 1])
        brow = sb("brow", [128, 4, 128])
        table_in = sb("table_in", [128, 1])
        table_out = sb("table_out", [128, 6])
        rw2p = sb("rw2p", [128, 32])

        keys_bd = [sb(f"keys_bd{r}", [128, 4, HT, 128], f32r) for r in range(2)]
        values = [sb(f"values{r}", [128, 128]) for r in range(2)]
        probs = [work[:, 4096 + 1024 * u:5120 + 1024 * u].rearrange("p (h k) -> p h k", h=8) for u in (0, 1)]
        probs_t = [work[:, 6144 + 512 * i:6656 + 512 * i] for i in range(4)]
        neg_max = [sb(f"neg_max{u}", [128, 8]) for u in range(2)]
        sums = [sb(f"sums{r}", [128, H]) for r in range(2)]
        rec_small = sb("rec_small", [128, H])
        rec = [sb(f"rec{r}", [128, H, HD]) for r in range(2)]
        rec_t = [sb(f"rec_t{r}", [128, 128]) for r in range(2)]
        heads = [sb(f"heads{r}", [128, HT, 128]) for r in range(2)]

        bn6 = sb("bn6", [128, B, 6])
        mv = sb("mv", [128, B, 2])
        var = sb("var", [128, B])
        rs = sb("rs", [128, B])
        tmp = sb("tmp", [128, B])
        rsi = sb("rsi", [128, B], i32)
        normed4 = sb("normed4", [128, HT, 128])
        normed4_t = sb("normed4_t", [128, HT, 128])
        ctx4 = sb("ctx4", [128, HT, 128])
        lneg = sb("lneg", [128, NG])
        zsum = sb("zsum", [128, NG])
        top = sb("top", [128, NG, CAP])
        tsum = sb("tsum", [128, NG])
        ones = sb("ones", [128, NG, 128])
        def by_group(area, i):
            return area[:, 512 * i:512 * i + 512].rearrange("p (g t) -> p g t", g=NG)
        norm_t = [by_group(kv, g) for g in range(NG)]
        hid = [by_group(kv, NG + g) for g in range(NG)]
        probs_e, left, picked = [by_group(kv, 2 * NG + i) for i in range(3)]
        norm = work[:, 0:2048].rearrange("p (b d) -> p b d", b=B)
        place = [by_group(work, 4 + i) for i in range(2)]
        place_t = [by_group(work, 6 + i) for i in range(2)]
        sel = [sb(f"sel{r}", [128, E, CAP]) for r in range(4)]
        selw = [sb(f"selw{r}", [128, E, CAP]) for r in range(3)]
        scatter = late[:, :].rearrange("p (b m t) -> p b m t", b=B, m=4)
        exp_in = kv[:, :].rearrange("p (e b c) -> p e b c", e=E, b=B)
        exp_out = work[:, :].rearrange("p (b m d) -> p b m d", b=B, m=4)
        exp_out_g = work[:, :].rearrange("p (g b m d) -> p g b m d", g=NG, b=HT, m=4)
        ws = [sb(f"ws{r}", [128, 3 * F]) for r in range(4)]
        w1s = [w[:, 0:F] for w in ws]
        w2s = [w[:, F:2 * F] for w in ws]
        w3s = [w[:, 2 * F:3 * F].rearrange("p (m d) -> p m d", m=MT) for w in ws]
        gate_s = [sb(f"gate_s{m}", [128, 512]) for m in range(MT)]
        act_s = [sb(f"act_s{r}", [128, MT, 512]) for r in range(2)]
        y_s = [sb(f"y_s{r}", [128, NG, 128]) for r in range(2)]

        score_p = ps("score_p", [128, 4, HT, 128])
        turn_p = [ps(f"turn_p{i}", [128, HT, 128]) for i in range(2)]
        heads_p = ps("heads_p", [128, HT, 128])
        aux_p = ps("aux_p", [128, HT, 128])
        banks = [score_p[:, i] for i in range(4)] + [turn_p[0][:], turn_p[1][:], heads_p[:], aux_p[:]]

        s_x = [sem(f"s_x{g}") for g in range(NG)]
        s_const = sem("s_const")
        s_ctx = sem("s_ctx")
        s_ctx4 = sem("s_ctx4")
        s_dve_const = sem("s_dve_const")
        s_pool_const = sem("s_pool_const")
        s_stats = sem("s_stats")
        s_rs = sem("s_rs")
        s_n4 = sem("s_n4")
        s_n4t = sem("s_n4t")
        s_n4c = sem("s_n4c")
        s_qp = sem("s_qp")
        s_kp = sem("s_kp")
        s_vp = sem("s_vp")
        s_qk_out = sem("s_qk_out")
        s_split = sem("s_split")
        s_q_written = sem("s_q_written")
        s_k_written = sem("s_k_written")
        s_q_stack = [sem(f"s_q_stack{b}") for b in range(HT)]
        s_k_stack = sem("s_k_stack")
        s_v_out = sem("s_v_out")
        s_biased = sem("s_biased")
        s_keys = sem("s_keys")
        s_v = sem("s_v")
        s_scored = sem("s_scored")
        s_maxed = sem("s_maxed")
        s_exped = sem("s_exped")
        s_rec = sem("s_rec")
        s_rec_turned = sem("s_rec_turned")
        s_rec_copied = sem("s_rec_copied")
        s_turned = sem("s_turned")
        s_turn_copied = sem("s_turn_copied")
        s_turn3_copied = sem("s_turn3_copied")
        s_mixed = sem("s_mixed")
        s_heads = sem("s_heads")
        s_projected = sem("s_projected")
        s_added = sem("s_added")
        s_norm = sem("s_norm")
        s_norm3 = sem("s_norm3")
        s_norm_t = sem("s_norm_t")
        s_norm_tc = sem("s_norm_tc")
        s_hid = sem("s_hid")
        s_hid_s = sem("s_hid_s")
        s_logits = sem("s_logits")
        s_lmax = sem("s_lmax")
        s_lexp = sem("s_lexp")
        s_place = sem("s_place")
        s_place_t = sem("s_place_t")
        s_place_c = sem("s_place_c")
        s_sel = sem("s_sel")
        s_selw = sem("s_selw")
        s_gathered = sem("s_gathered")
        s_gat_copied = sem("s_gat_copied")
        s_scat = sem("s_scat")
        s_scat_copied = sem("s_scat_copied")
        s_w = [sem(f"s_w{r}") for r in range(4)]
        s_gate = sem("s_gate")
        s_value = sem("s_value")
        s_silu = sem("s_silu")
        s_act = sem("s_act")
        s_y = sem("s_y")
        s_yc = sem("s_yc")
        s_yd = [sem(f"s_yd{r}") for r in range(2)]
        s_comb = sem("s_comb")
        s_fin = sem("s_fin")
        s_out = sem("s_out")

        COMBINE_BANKS = (6, 7, 0, 1, 2, 3, 4, 5)

        turn_bank = (None, banks[1], banks[2], banks[4])
        hidden_bank = (banks[3], banks[1], banks[2], banks[5])
        scatter_bank = (banks[0], banks[3], banks[6], banks[7])
        logit_bank = (banks[0], banks[0], banks[0], banks[6])

        STACKED = 16 * 4
        CONSTS = 16 * 6

        block = ctx.enter_context(nc.Block())

        JOBS = 2 * B
        PREPS = JOBS // HT

        def at_least(n, least):
            return not isinstance(n, int) or n >= least

        def parts_of_slot(n):
            return not isinstance(n, int) or n < JOBS, not isinstance(n, int) or 1 <= n <= JOBS, at_least(n, 2)

        def steps(engine, step, slot):
            step(0)
            with engine.Fori(1, 3) as k:
                step(k, SELF)
            step(3)
            step(4)
            with engine.Fori(5, 7) as k:
                step(k, CROSS)
            step(7)
            slot(JOBS, 0, PREPS)
            slot(JOBS + 1, 1, PREPS)

        SELF, CROSS = 0, 1
        KEYS, QUERIES, VALUES, TURN = range(4)

        def kind_of(n, kind):
            return kind if not isinstance(n, int) else SELF if n < B else CROSS

        def has_next(k):
            return not isinstance(k, int) or k < PREPS - 1

        def next_kind(k, kind):
            return kind if not isinstance(k, int) else SELF if k + 1 < NG else CROSS

        def batches_of(q, kind):
            return (q if kind == SELF else q - NG) * HT

        def batches_ahead(k, kind):
            return (k + 2) % NG * HT if isinstance(k, int) else ((2 if kind == SELF else 6) - k) * (B - HT)

        def parity(k, kind):
            return k % 2 if isinstance(k, int) else k * -1 + (2 if kind == SELF else 6)

        def next_parity(k, kind):
            return (k + 1) % 2 if isinstance(k, int) else k - (1 if kind == SELF else 5)

        def newton(vector, engine, cols, fused):
            v, y, w = var[:, cols], rs[:, cols], tmp[:, cols]
            for i in range(NEWTON):
                if i > 0:
                    engine.drain()
                vector.tensor_tensor(w, y, y, ALU.mult)
                engine.drain()
                if fused:
                    vector.scalar_tensor_tensor(w, w, -0.5, v, ALU.mult, ALU.mult)
                    engine.drain()
                    last = vector.scalar_tensor_tensor(y, w, 1.5, y, ALU.add, ALU.mult)
                else:
                    vector.tensor_tensor(w, w, v, ALU.mult)
                    engine.drain()
                    vector.tensor_scalar(w, w, -0.5, 1.5, ALU.mult, ALU.add)
                    engine.drain()
                    last = vector.tensor_tensor(y, y, w, ALU.mult)
            return last

        @block.sync
        def _(sp):
            for g in range(NG):
                sp.dma_start(resid[:, HT * g:HT * g + HT, :],
                             x[HT * g:HT * g + HT].rearrange("b s d -> s b d")).then_inc(s_x[g], 16)
                if g == 0:
                    sp.dma_start(cst[:], consts).then_inc(s_const, 16)
                    sp.dma_start(wt[:], weights).then_inc(s_const, 16)
                    sp.dma_start(maskf[:], masks).then_inc(s_const, 16)
                    sp.dma_start(bcol[:], bias_cols).then_inc(s_const, 16)
                    sp.dma_start(brow[:], bias_rows).then_inc(s_const, 16)
            sp.wait_ge(s_pool_const, 1)
            sp.dma_start(rw2p[:, 0:E], rw2).then_inc(s_const, 16)
            sp.dma_start(ctx_all, ctx_t).then_inc(s_ctx, 16)

            def write_parts(q, i):
                sp.wait_ge(s_split, q * 2 + i + 1)
                sp.dma_start(scratch[i], (k_parts, q_parts)[i]).then_inc((s_k_written, s_q_written)[i], 16)

            def stack_keys(q, r):
                if at_least(q, 2):
                    sp.wait_ge(s_keys, q * 4 - 4)
                sp.wait_ge(s_k_written, q * 16 + 16)
                for s in range(4):
                    sp.dma_start(k_stack[32 * s:32 * s + 32, r].rearrange("p g b t -> p g (b t)"),
                                 scratch[KEYS, :, (0, 1, 0, 1)[s], :].rearrange("(g p) t -> p g t", g=4)).then_inc(s_k_stack, 16)

            def stack_queries(q):
                sp.wait_ge(s_q_written, q * 16 + 16)
                for b in range(HT):
                    if at_least(q, 1):
                        sp.wait_ge(s_scored, (q * 4 + b) * 2 - 6)
                    for s in range(4):
                        sp.dma_start(q_stack[b][32 * s:32 * s + 32],
                                     scratch[QUERIES, :, (0, 0, 1, 1)[s], 128 * b:128 * b + 128]
                                     .rearrange("(g p) t -> p g t", g=4)).then_inc(s_q_stack[b], 16)

            def stack(q, r):
                write_parts(q, KEYS)
                stack_keys(q, r)
                write_parts(q, QUERIES)
                stack_queries(q)

            write_parts(0, KEYS)
            write_parts(0, QUERIES)
            stack_keys(0, 0)
            stack_queries(0)
            stack(1, 1)
            with sp.Fori(1, PREPS // 2) as q2:
                for r in range(2):
                    stack(q2 * 2 + r, r)

            def load(e, e4):
                sp.dma_start(ws[e4][:], expert_w[e]).then_inc(s_w[e4], 16)

            def spread(m, e4):
                sp.wait_ge(s_yc, m * 4 + e4 + 1)
                for b4 in range(HT):
                    dst = exp_out_g[CAP * e4:CAP * e4 + CAP, :, b4, m, :]
                    sp.dma_start(dst, y_s[e4 % 2][CAP * b4:CAP * b4 + CAP, :, :]).then_inc(s_yd[e4 % 2], 16)

            for e4 in range(4):
                load(e4, e4)
            with sp.Fori(0, E // 4 - 1) as m:
                for e4 in range(4):
                    sp.wait_ge(s_y, m * 4 + e4 + 1)
                    load(m * 4 + e4 + 4, e4)
                    spread(m, e4)
            for e4 in range(4):
                spread(E // 4 - 1, e4)
            for g in range(NG):
                sp.wait_ge(s_fin, NG + g + 1)
                sp.dma_start(out[HT * g:HT * g + HT].rearrange("b s d -> s b d"),
                             resid[:, HT * g:HT * g + HT, :]).then_inc(s_out, 16)
            sp.wait_ge(s_out, 16 * NG)

        @block.tensor
        def _(pe):
            pe.wait_ge(s_const, CONSTS)

            def piece(q, i, kind, bank):
                wq, wk, wv = (WQ, WK, WV) if kind == SELF else (XQ, XK, XV)
                source = normed4_t if kind == SELF else ctx4
                if i == TURN:
                    pe.wait_ge(s_n4, q + 1)
                    for b in range(HT):
                        last = nc.tensor.transpose(bank[:, b, :], normed4[:, b, :], ident)
                    last.then_inc(s_n4t, 1)
                elif i == QUERIES:
                    pe.wait_ge(s_n4c, q + 1)
                    nc.tensor.matmul(bank, wt[:, wq, :], normed4_t[:], start=True, stop=True).then_inc(s_qp, 1)
                elif i == KEYS:
                    if kind == CROSS:
                        pe.wait_ge(s_ctx4, q - NG + 1)
                    else:
                        pe.wait_ge(s_n4c, q + 1)
                    nc.tensor.matmul(bank, wt[:, wk, :], source[:], start=True, stop=True).then_inc(s_kp, 1)
                else:
                    for b in range(HT):
                        last = nc.tensor.matmul(bank[:, b, :], source[:, b, :], wt[:, wv, :], start=True, stop=True)
                    last.then_inc(s_vp, 1)

            for i, which in enumerate((TURN, KEYS, QUERIES, VALUES)):
                piece(0, which, SELF, banks[i])
            piece(1, TURN, SELF, aux_p[:])
            pe.wait_ge(s_dve_const, 1)

            def score(n, b, u, kind):
                if at_least(n, 1):
                    pe.wait_ge(s_exped, n * 2 + u - 1)
                elif u == 0:
                    pe.wait_ge(s_qk_out, 2)
                    pe.wait_ge(s_v_out, 1)
                if u == 0:
                    pe.wait_ge(s_keys, n + 1)
                    pe.wait_ge(s_q_stack[b], (n - b) * (STACKED // HT) + STACKED)
                for i in (2 * u, 2 * u + 1):
                    nc.tensor.matmul(score_p[:, i], ident_b[:], mask_b[kind][:], start=True, stop=False)
                    last = nc.tensor.matmul(score_p[:, i], q_stack[b][:, i, :].bitcast(f32r), keys_bd[b % 2][:, i, :, :],
                                            start=False, stop=True)
                last.then_inc(s_scored, 1)

            def turn(n, g):
                if g % 2 == 0:
                    pe.wait_ge(s_exped, n * 2 + g // 2 + 1)
                if g >= 2:
                    pe.wait_ge(s_turn_copied, n * 3 + g - 1)
                elif at_least(n, 1):
                    pe.wait_ge((s_turn_copied, s_turn3_copied)[g], (n * 3, n)[g])
                for j in range(HT):
                    last = nc.tensor.transpose(turn_p[g % 2][:, j, :], probs[g // 2][:, HT * (g % 2) + j, :], ident)
                last.then_inc(s_turned, 1)

            def mix(n, r, g):
                if g == 0:
                    pe.wait_ge(s_v, n + 1)
                    if at_least(n, 1):
                        pe.wait_ge(s_added, n)
                if g < 3:
                    pe.wait_ge(s_turn_copied, n * 3 + g + 1)
                else:
                    pe.wait_ge(s_turn3_copied, n + 1)
                rows = slice(32 * g, 32 * g + 32)
                last = nc.tensor.matmul(heads_p[rows], values[r][:, rows], probs_t[g], start=True, stop=True)
                if g == 3:
                    last.then_inc(s_mixed, 1)

            def turn_rec(n, r, b, k):
                pe.wait_ge(s_rec, n + 1)
                if b == 0 and not (isinstance(k, int) and k == PREPS):
                    pe.wait_ge(s_n4c, k + 2)
                elif not has_next(k):
                    pe.wait_ge(s_rec_copied, n)
                elif b == VALUES + 1:
                    pe.wait_ge(s_v_out, k + 2)
                else:
                    pe.wait_ge(s_qk_out, k * 2 + 2 + b)
                nc.tensor.transpose(aux_p[:, 0, :], rec[r][:].rearrange("p h i -> p (h i)"), ident).then_inc(s_rec_turned, 1)

            def project(n, r, kind):
                pe.wait_ge(s_heads, n + 1)
                for j in range(HT):
                    last = nc.tensor.matmul(heads_p[:, 0, :], heads[r][:, j, :], wo_own[kind][:, j, :],
                                            start=(j == 0), stop=(j == HT - 1))
                last.then_inc(s_projected, 1)

            def slot(n, b, k, kind=None):
                r = b % 2
                scores, mixes, projects = parts_of_slot(n)
                if scores:
                    score(n, b, 0, kind_of(n, kind))
                if projects:
                    project(n - 2, r, kind_of(n - 2 if isinstance(n, int) else n, kind))
                if mixes:
                    turn(n - 1, 0)
                    turn(n - 1, 1)
                if scores:
                    score(n, b, 1, kind_of(n, kind))
                if mixes:
                    turn_rec(n - 1, 1 - r, b, k)
                    mix(n - 1, 1 - r, 0)
                    mix(n - 1, 1 - r, 1)
                    turn(n - 1, 2)
                    turn(n - 1, 3)
                if has_next(k) and scores:
                    if mixes:
                        pe.wait_ge(s_rec_copied, n)
                    piece(k + 2 if b == TURN else k + 1, b, next_kind(k, kind), aux_p[:])
                if mixes:
                    mix(n - 1, 1 - r, 2)
                    mix(n - 1, 1 - r, 3)

            def step(k, kind=None):
                for b in range(HT):
                    slot(k * HT + b, b, k, kind)

            steps(pe, step, slot)

            def turn_tokens(g):
                if g < NG - 1:
                    pe.wait_ge(s_norm, g)
                else:
                    pe.wait_ge(s_norm3, 1)
                for b in range(HT):
                    last = nc.tensor.transpose(turn_bank[g][:, b, :], norm[:, HT * g + b, :], ident)
                last.then_inc(s_norm_t, 1)

            def hidden(g):
                if g == 0:
                    pe.wait_ge(s_n4c, PREPS + 1)
                else:
                    pe.wait_ge(s_norm_tc, g)
                tokens = norm_t[g] if g > 0 else normed4_t[:]
                nc.tensor.matmul(hidden_bank[g], wt[:, RW1, :], tokens, start=True, stop=True).then_inc(s_hid, 1)

            def logits(g):
                pe.wait_ge(s_hid_s, g + 1)
                for b in range(HT):
                    last = nc.tensor.matmul(logit_bank[g][32 * b:32 * b + 32, g, :], rw2p[:], hid[g][:, b, :],
                                            start=True, stop=True)
                last.then_inc(s_logits, 1)

            pe.wait_ge(s_exped, JOBS * 2)
            hidden(0)
            for g in range(1, NG - 1):
                turn_tokens(g)
            for g in range(1, NG - 1):
                hidden(g)
            for g in range(NG - 1):
                logits(g)
            turn_tokens(NG - 1)
            hidden(NG - 1)
            logits(NG - 1)
            for i in range(2):
                pe.wait_ge(s_place, i + 1)
                for g in range(NG):
                    last = nc.tensor.transpose(banks[1 + i][:, g, :], place[i][:, g, :], ident)
                last.then_inc(s_place_t, 1)

            def gather(b):
                pe.wait_ge(s_sel, b + 1)
                if b >= 2:
                    pe.wait_ge(s_gat_copied, b - 1)
                nc.tensor.matmul(banks[4 + b % 2], norm[:, b, :], sel[b % 4][:], start=True, stop=True).then_inc(s_gathered, 1)

            pe.wait_ge(s_norm, 3)
            gather(0)
            for b in range(B):
                if b < B - 1:
                    gather(b + 1)
                pe.wait_ge(s_selw, b + 1)
                if b >= 4:
                    pe.wait_ge(s_scat_copied, b - 3)
                for m in range(4):
                    last = nc.tensor.transpose(scatter_bank[b % 4][:, m, :], selw[b % 3][:, 4 * m:4 * m + 4, :], ident)
                last.then_inc(s_scat, 1)

            def gate_value(e, e4):
                pe.wait_ge(s_w[e4], (e - e4) * 4 + 16)
                for m in range(MT):
                    if not (isinstance(e, int) and e == 0):
                        pe.wait_ge(s_act, e * MT + m - 1)
                    cols = slice(128 * m, 128 * m + 128)
                    nc.tensor.matmul(banks[m], w1s[e4][:, cols], exp_in[:, e], start=True, stop=True).then_inc(s_gate, 1)
                    nc.tensor.matmul(banks[2 + m], w2s[e4][:, cols], exp_in[:, e], start=True, stop=True).then_inc(s_value, 1)

            def outputs(e, e4):
                r = e4 % 2
                pe.wait_ge(s_act, e * MT + MT)
                if not (isinstance(e, int) and e < 2):
                    pe.wait_ge(s_yc, e - 1)
                for g in range(NG):
                    for m in range(MT):
                        last = nc.tensor.matmul(banks[4 + r][:, g, :], act_s[r][:, m, 128 * g:128 * g + 128],
                                                w3s[e4][:, m, :], start=(m == 0), stop=(m == MT - 1))
                last.then_inc(s_y, 1)

            pe.wait_ge(s_gat_copied, B)
            pe.wait_ge(s_scat_copied, B - 2)
            gate_value(0, 0)
            for e4 in range(3):
                gate_value(e4 + 1, e4 + 1)
                outputs(e4, e4)
            with pe.Fori(1, E // 4) as m4:
                for e4 in range(4):
                    gate_value(m4 * 4 + e4, e4)
                    outputs(m4 * 4 + e4 - 1, (e4 + 3) % 4)
            outputs(E - 1, 3)

            def combine(g, bank, ms):
                for b in range(HT):
                    for m in ms:
                        last = nc.tensor.matmul(banks[bank][:, b, :], scatter[:, HT * g + b, m, :], exp_out[:, HT * g + b, m, :],
                                                start=(m == ms[0]), stop=(m == ms[-1]))
                last.then_inc(s_comb, 1)

            pe.wait_ge(s_act, E * MT)
            for r in range(2):
                pe.wait_ge(s_yd[r], 16 * HT * 6)
            pe.wait_ge(s_scat_copied, B)
            for g in range(NG):
                combine(g, COMBINE_BANKS[g], (0, 1, 2))
            for r in range(2):
                pe.wait_ge(s_yd[r], 16 * HT * 8)
            for g in range(NG):
                combine(g, COMBINE_BANKS[NG + g], (3,))

        @block.scalar
        def _(act):
            def load_table(i, function):
                nc.scalar.activation(table_out[:, i:i + 1], table_in[:], function)

            act.wait_ge(s_pool_const, 1)
            load_table(0, ACT.Exp)
            act.wait_ge(s_const, CONSTS)

            def piece(q, i, kind, bank):
                if i == TURN:
                    act.wait_ge(s_n4t, q + 1)
                    if at_least(q, 1):
                        act.wait_ge(s_qp, q)
                        act.wait_ge(s_vp, q)
                    nc.scalar.copy(normed4_t[:], bank).then_inc(s_n4c, 1)
                elif i in (QUERIES, KEYS):
                    done, stacked = ((s_kp, [s_k_stack]), (s_qp, s_q_stack))[i]
                    act.wait_ge(done, q + 1)
                    if at_least(q, 1):
                        for stack in stacked:
                            act.wait_ge(stack, q * STACKED)
                    to, bank = (k_parts, q_parts)[i][:, 1, :], bank.rearrange("p b t -> p (b t)")
                    if kind == SELF:
                        last = nc.scalar.activation(to, bank, ACT.Identity, bias=(bcol[:, 1:2], bq_scaled[:])[i],
                                                    scale=(1.0, SCALE)[i])
                    else:
                        last = nc.scalar.activation(to, bank, ACT.Copy, scale=(1.0, SCALE)[i])
                    last.then_inc(s_qk_out, 1)

            piece(0, TURN, SELF, banks[0])
            act.wait_ge(s_dve_const, 1)
            piece(0, KEYS, SELF, banks[1])
            piece(0, QUERIES, SELF, banks[2])
            piece(1, TURN, SELF, aux_p[:])

            def exps(n, r, u):
                act.wait_ge(s_maxed, n * 2 + u + 1)
                if at_least(n, 1):
                    act.wait_ge(s_turned, n * 4 + 2 * u - 2)
                if at_least(n, 2) and u == 0:
                    act.wait_ge(s_rec, n - 1)
                for h in range(8):
                    last = nc.scalar.activation(probs[u][:, h, :], score_p[:, 2 * u + h // HT, h % HT, :], ACT.Exp,
                                                bias=neg_max[u][:, h:h + 1], accum_out=sums[r][:, 8 * u + h:8 * u + h + 1])
                last.then_inc(s_exped, 1)

            def slot(n, b, k, kind=None):
                scores, mixes, _ = parts_of_slot(n)
                if scores:
                    exps(n, b % 2, 0)
                if mixes:
                    act.wait_ge(s_rec_turned, n)
                    if at_least(n, 3):
                        act.wait_ge(s_heads, n - 2)
                    nc.scalar.copy(rec_t[1 - b % 2][:], aux_p[:, 0, :]).then_inc(s_rec_copied, 1)
                if mixes:
                    act.wait_ge(s_turned, n * 4)
                    nc.scalar.copy(probs_t[3], turn_p[1][:].rearrange("p a b -> p (a b)")).then_inc(s_turn3_copied, 1)
                if scores:
                    exps(n, b % 2, 1)
                    if has_next(k) and b != VALUES:
                        piece(k + 2 if b == TURN else k + 1, b, next_kind(k, kind), aux_p[:])

            def step(k, kind=None):
                for b in range(HT):
                    slot(k * HT + b, b, k, kind)

            steps(act, step, slot)

            def copy_tokens(g):
                act.wait_ge(s_norm_t, g)
                nc.scalar.copy(norm_t[g], turn_bank[g]).then_inc(s_norm_tc, 1)

            def silu_hidden(g):
                act.wait_ge(s_hid, g + 1)
                nc.scalar.activation(hid[g], hidden_bank[g], ACT.Silu).then_inc(s_hid_s, 1)

            def exp_logits(g):
                act.wait_ge(s_lmax, 1 if g < NG - 1 else 2)
                nc.scalar.activation(probs_e[:, g, :], logit_bank[g][:, g, :], ACT.Exp, bias=lneg[:, g:g + 1],
                                     accum_out=zsum[:, g:g + 1]).then_inc(s_lexp, 1)

            load_table(1, ACT.Silu)
            for g in range(1, NG - 1):
                copy_tokens(g)
            for g in range(NG - 1):
                silu_hidden(g)
            load_table(2, ACT.Exp)
            for g in range(NG - 1):
                exp_logits(g)
            load_table(3, ACT.Silu)
            copy_tokens(NG - 1)
            silu_hidden(NG - 1)
            load_table(4, ACT.Exp)
            exp_logits(NG - 1)
            load_table(5, ACT.Silu)
            act.wait_ge(s_place_t, 2)
            nc.scalar.copy(place_t[1], banks[2]).then_inc(s_place_c, 1)
            with act.Fori(0, B // 2) as b2:
                for r in range(2):
                    act.wait_ge(s_gathered, b2 * 2 + r + 1)
                    nc.scalar.copy(exp_in[:, :, b2 * 2 + r, :],
                                   banks[4 + r].rearrange("p a b -> p (a b)").rearrange("p (e c) -> p e c", e=E)
                                   ).then_inc(s_gat_copied, 1)

            def silu(e):
                for m in range(MT):
                    act.wait_ge(s_gate, e * MT + m + 1)
                    if not (isinstance(e, int) and e == 0):
                        act.wait_ge(s_act, e * MT + m - 1)
                    nc.scalar.activation(gate_s[m][:], banks[m], ACT.Silu).then_inc(s_silu, 1)

            def copy_out(e, e4):
                act.wait_ge(s_y, e + 1)
                if not (isinstance(e, int) and e < 2):
                    act.wait_ge(s_yd[e4 % 2], (e - e4) * 8 * HT + 16 * HT * (e4 // 2))
                nc.scalar.copy(y_s[e4 % 2][:], banks[4 + e4 % 2]).then_inc(s_yc, 1)

            silu(0)
            for e4 in range(3):
                silu(e4 + 1)
                copy_out(e4, e4)
            with act.Fori(1, E // 4) as m4:
                for e4 in range(4):
                    silu(m4 * 4 + e4)
                    copy_out(m4 * 4 + e4 - 1, (e4 + 3) % 4)
            copy_out(E - 1, 3)

        @block.gpsimd
        def _(pool):
            nc.gpsimd.memset(table_in[:], 0.0)
            nc.gpsimd.memset(rw2p[:], 0.0).then_inc(s_pool_const, 1)
            nc.gpsimd.memset(ones[:, :, 1:128], 1.0)
            nc.gpsimd.memset(ones[:, :, 0:1], 0.0).then_inc(s_pool_const, 1)

            def add_bias(q, kind):
                pool.wait_ge(s_n4, q + 1)
                group = resid[:, bass.ds(batches_of(q, kind), HT), :]
                row = brow[:, BO if kind == SELF else XBO, :].unsqueeze(1).broadcast_to([128, HT, 128])
                nc.gpsimd.tensor_tensor(group, group, row, ALU.add).then_inc(s_biased, 1)

            def fetch_keys(n, r, b, stacked, ring):
                pool.wait_ge(s_k_stack, stacked * STACKED)
                if at_least(n, 2):
                    pool.wait_ge(s_scored, n * 2 - 2)
                nc.gpsimd.tensor_tensor(keys_bd[r][:], k_stack[:, ring, :, b, :].unsqueeze(2).broadcast_to([128, 4, HT, 128]),
                                        own.unsqueeze(1).unsqueeze(3).broadcast_to([128, 4, HT, 128]), ALU.mult
                                        ).then_inc(s_keys, 1)

            def fetch_values(n, r, kind, k):
                pool.wait_ge(s_v_out, k + 1)
                if at_least(n, 2):
                    pool.wait_ge(s_mixed, n - 1)
                nc.gpsimd.tensor_copy(values[r][:], vt[:, n if kind == SELF else n - B, :]).then_inc(s_v, 1)

            pool.wait_ge(s_const, CONSTS)
            fetch_keys(0, 0, 0, 1, 0)
            add_bias(0, SELF)

            def step(k, kind=None):
                for b in range(HT):
                    n = k * HT + b
                    fetch_values(n, b % 2, kind_of(n, kind), k)
                    if b == 0 and has_next(k) and next_kind(k, kind) == CROSS:
                        group = ctx_all[:, bass.ds(k + 1 - NG, 1), :]
                        pool.wait_ge(s_ctx, 16)
                        nc.gpsimd.tensor_copy(ctx4[:].rearrange("p b t -> p (b t)").unsqueeze(1), group).then_inc(s_ctx4, 1)
                    if b < 3:
                        fetch_keys(n + 1, (b + 1) % 2, b + 1, k + 1, parity(k, kind))
                    elif has_next(k):
                        fetch_keys(n + 1, 0, 0, k + 2, next_parity(k, kind))
                    if b == 3 and not has_next(k):
                        pool.wait_ge(s_stats, k + 1)
                        newton(nc.gpsimd, pool, slice(0, 3 * HT), fused=False).then_inc(s_rs, 1)
                        pool.wait_ge(s_rs, PREPS)
                        for g in (1, 2, 0):
                            for i in range(HT * g, HT * g + HT):
                                last = nc.gpsimd.tensor_scalar(norm[:, i, :], resid[:, i, :], mv[:, i, 0:1], rs[:, i:i + 1],
                                                               ALU.subtract, ALU.mult)
                            last.then_inc(s_norm, 1)
                    if b == 2 and has_next(k):
                        pool.wait_ge(s_stats, k + 1)
                        newton(nc.gpsimd, pool, slice(0, HT), fused=False).then_inc(s_rs, 1)
                    if b == 3 and has_next(k):
                        add_bias(k + 1, next_kind(k, kind))

            def no_slot(n, b, k):
                pass

            steps(pool, step, no_slot)

            pool.wait_ge(s_place_c, 1)
            for b in range(B):
                pool.wait_ge(s_sel, b + 1)
                if b >= 3:
                    pool.wait_ge(s_scat, b - 2)
                weight = place_t[1][:, b // HT, 32 * (b % HT):32 * (b % HT) + E]
                nc.gpsimd.tensor_tensor(selw[b % 3][:], sel[b % 4][:], weight.unsqueeze(2).broadcast_to([128, E, CAP]),
                                        ALU.mult).then_inc(s_selw, 1)

        @block.vector
        def _(dve):
            def stats(first, col):
                for i in range(HT):
                    nc.vector.bn_stats(bn6[:, col + i, :], resid[:, first + i, :])
                dve.drain()
                for i in range(HT):
                    nc.vector.bn_aggr(mv[:, col + i, :], bn6[:, col + i, :])

            def first_guess(cols):
                v, i = var[:, cols], rsi[:, cols]
                dve.drain()
                nc.vector.tensor_scalar(v, mv[:, cols, 1], EPS, None, ALU.add)
                dve.drain()
                nc.vector.tensor_scalar(i, v.bitcast(i32), 1, None, ALU.logical_shift_right)
                dve.drain()
                return nc.vector.tensor_scalar(rs[:, cols].bitcast(i32), i, -1.0, float(RSQRT_MAGIC), ALU.mult, ALU.add)

            def rsqrt(cols):
                first_guess(cols)
                dve.drain()
                newton(nc.vector, dve, cols, fused=True)
                dve.drain()

            def normalise(first, col, target=None, count=0):
                if not (isinstance(count, int) and count == 0):
                    dve.wait_ge(s_n4t, count)
                for b in range(HT):
                    last = nc.vector.tensor_scalar((normed4 if target is None else target)[:, b, :], resid[:, first + b, :],
                                                   mv[:, bass.ds(col + b, 1), 0], rs[:, bass.ds(col + b, 1)], ALU.subtract, ALU.mult)
                return last

            dve.wait_ge(s_x[0], 16)
            stats(0, 0)
            rsqrt(slice(0, HT))
            normalise(0, 0).then_inc(s_n4, 1)
            dve.wait_ge(s_const, CONSTS)
            nc.vector.tensor_copy(ident_b[:], maskf[:, 0, :])
            for i in range(2):
                nc.vector.tensor_copy(mask_b[i][:], maskf[:, 1 + i, :].unsqueeze(1).broadcast_to([128, HT, 128]))
            for i, w in enumerate((WO, XO)):
                last = nc.vector.tensor_tensor(wo_own[i][:], wt[:, w, :].unsqueeze(1).broadcast_to([128, HT, 128]),
                                               own.unsqueeze(2).broadcast_to([128, HT, 128]), ALU.mult)
            nc.vector.tensor_scalar(bq_scaled[:], bcol[:, 0:1], SCALE, None, ALU.mult).then_inc(s_dve_const, 1)

            def values_out(q, kind, bank):
                dve.wait_ge(s_vp, q + 1)
                row = brow[:, BV if kind == SELF else XBV, :].unsqueeze(1).broadcast_to([128, HT, 128])
                nc.vector.tensor_tensor(vt[:, bass.ds(batches_of(q, kind), HT), :], bank, row, ALU.add).then_inc(s_v_out, 1)

            def split(q, i):
                parts = (k_parts, q_parts)[i]
                dve.wait_ge(s_qk_out, q * 2 + i + 1)
                high, low = parts[:, 0, :], parts[:, 1, :]
                nc.vector.tensor_scalar(high.bitcast(i32), low.bitcast(i32), LOW_BITS, LOW_BITS,
                                        ALU.logical_shift_right, ALU.logical_shift_left)
                dve.drain()
                nc.vector.tensor_tensor(low, low, high, ALU.subtract).then_inc(s_split, 1)

            split(0, KEYS)
            split(0, QUERIES)
            values_out(0, SELF, banks[3])
            for g in range(1, NG):
                dve.wait_ge(s_x[g], 16)
            stats(HT, 0)
            rsqrt(slice(0, HT))
            normalise(HT, 0, count=1).then_inc(s_n4, 1)

            def maximum(n, u):
                dve.wait_ge(s_scored, n * 2 + u + 1)
                nc.vector.tensor_reduce(neg_max[u][:], score_p[:, 2 * u:2 * u + 2].rearrange("p a h k -> p (a h) k"),
                                        AX.X, ALU.max, negate=True).then_inc(s_maxed, 1)

            def copy_turned(n, g):
                dve.wait_ge(s_turned, n * 4 + g + 1)
                nc.vector.tensor_copy(probs_t[g], turn_p[g % 2][:].rearrange("p a b -> p (a b)")).then_inc(s_turn_copied, 1)

            def slot(n, b, k, kind=None):
                r = b % 2
                scores, mixes, projects = parts_of_slot(n)
                ahead = scores and has_next(k)
                if scores:
                    maximum(n, 0)
                if mixes:
                    dve.wait_ge(s_exped, n * 2)
                    nc.vector.reciprocal(rec_small[:], sums[1 - r][:])
                    dve.drain()
                    if at_least(n, 3):
                        dve.wait_ge(s_rec_turned, n - 2)
                    nc.vector.tensor_copy(rec[1 - r][:], rec_small[:].unsqueeze(2).broadcast_to([128, H, HD])).then_inc(s_rec, 1)
                if projects:
                    batch = n - 2 if kind_of(n - 2 if isinstance(n, int) else n, kind) == SELF else n - 2 - B
                    if b == 2:
                        dve.wait_ge(s_biased, k + 1)
                    dve.wait_ge(s_projected, n - 1)
                    nc.vector.tensor_tensor(resid[:, batch, :], heads_p[:, 0, :], resid[:, batch, :], ALU.add).then_inc(s_added, 1)
                if mixes:
                    copy_turned(n - 1, 0)
                    copy_turned(n - 1, 1)
                if ahead and b in (QUERIES + 1, KEYS + 1):
                    split(k + 1, b - 1)
                if scores:
                    maximum(n, 1)
                if ahead and b == 3:
                    dve.wait_ge(s_rs, k + 1)
                    normalise(batches_ahead(k, kind), 0, count=k + 2).then_inc(s_n4, 1)
                if mixes:
                    copy_turned(n - 1, 2)
                if ahead and b == VALUES:
                    values_out(k + 1, next_kind(k, kind), aux_p[:])
                if ahead and b == 0:
                    stats(batches_ahead(k, kind), 0)
                if ahead and b == 1:
                    first_guess(slice(0, HT)).then_inc(s_stats, 1)
                if mixes:
                    dve.wait_ge(s_rec_copied, n)
                    dve.wait_ge(s_mixed, n)
                    nc.vector.tensor_tensor(heads[1 - r][:], heads_p[:], rec_t[1 - r][:].unsqueeze(1).broadcast_to([128, HT, 128]),
                                            ALU.mult).then_inc(s_heads, 1)
                if scores and not has_next(k) and b < 3:
                    stats(b * HT, b * HT)
                    if b == 2:
                        first_guess(slice(0, 3 * HT)).then_inc(s_stats, 1)

            def step(k, kind=None):
                for b in range(HT):
                    slot(k * HT + b, b, k, kind)

            steps(dve, step, slot)

            dve.wait_ge(s_added, JOBS)
            stats(B - HT, B - HT)
            rsqrt(slice(B - HT, B))
            normalise(B - HT, B - HT, norm[:, B - HT:B]).then_inc(s_norm3, 1)

            def largest(groups):
                dve.wait_ge(s_logits, groups[-1] + 1)
                nc.vector.tensor_reduce(lneg[:, groups[0]:groups[-1] + 1], logit_bank[groups[0]][:, groups[0]:groups[-1] + 1, :],
                                        AX.X, ALU.max, negate=True).then_inc(s_lmax, 1)
                for i in range(CAP // 8):
                    source = probs_e if i == 0 else left
                    for g in groups:
                        if i == 0:
                            dve.wait_ge(s_lexp, g + 1)
                        nc.vector.max(top[:, g, 8 * i:8 * i + 8], source[:, g, :])
                    dve.drain()
                    for g in groups:
                        nc.vector.match_replace(left[:, g, :], top[:, g, 8 * i:8 * i + 8], source[:, g, :], -1.0)
                    dve.drain()

            largest(range(NG - 1))
            largest(range(NG - 1, NG))
            nc.vector.tensor_scalar(picked, left, 0.0, None, ALU.is_lt)
            nc.vector.reduce_sum(tsum[:], top[:], AX.X)
            dve.drain()
            dve.wait_ge(s_pool_const, 2)
            nc.vector.tensor_tensor_scan(left.rearrange("p g t -> p (g t)"), ones[:].rearrange("p g t -> p (g t)"),
                                         picked.rearrange("p g t -> p (g t)"), 0.0, ALU.mult, ALU.add)
            nc.vector.scalar_tensor_tensor(tsum[:], zsum[:], 1e-9, tsum[:], ALU.mult, ALU.add)
            dve.drain()
            nc.vector.tensor_tensor(place[0], left, picked, ALU.mult).then_inc(s_place, 1)
            nc.vector.reciprocal(tsum[:], tsum[:])
            dve.drain()
            for g in range(NG):
                last = nc.vector.scalar_tensor_tensor(place[1][:, g, :], probs_e[:, g, :], tsum[:, g:g + 1],
                                                      picked[:, g, :], ALU.mult, ALU.mult)
            last.then_inc(s_place, 1)
            dve.wait_ge(s_place_t, 1)
            nc.vector.tensor_copy(place_t[0], banks[1])
            dve.drain()

            def select(b):
                if b >= 4:
                    dve.wait_ge(s_selw, b - 3)
                    dve.wait_ge(s_gathered, b - 3)
                slots = place_t[0][:, b // HT, 32 * (b % HT):32 * (b % HT) + E]
                nc.vector.tensor_tensor(sel[b % 4][:], slots.unsqueeze(2).broadcast_to([128, E, CAP]),
                                        iota.unsqueeze(1).broadcast_to([128, E, CAP]), ALU.is_equal).then_inc(s_sel, 1)

            select(0)
            select(1)
            select(2)
            for b in range(B):
                if b < B - 3:
                    select(b + 3)
                dve.wait_ge(s_scat, b + 1)
                nc.vector.tensor_copy(scatter[:, b, :, :], scatter_bank[b % 4]).then_inc(s_scat_copied, 1)

            def activate(e, r):
                for m in range(MT):
                    dve.wait_ge(s_silu, e * MT + m + 1)
                    dve.wait_ge(s_value, e * MT + m + 1)
                    if not (isinstance(e, int) and e < 2):
                        dve.wait_ge(s_y, e - 1)
                    nc.vector.tensor_tensor(act_s[r][:, m, :], gate_s[m][:], banks[2 + m].rearrange("p a b -> p (a b)"),
                                            ALU.mult).then_inc(s_act, 1)

            activate(0, 0)
            activate(1, 1)
            with dve.Fori(1, E // 2) as e2:
                for r in range(2):
                    activate(e2 * 2 + r, r)

            for i in range(2 * NG):
                dve.wait_ge(s_comb, i + 1)
                if i >= NG:
                    dve.wait_ge(s_fin, i - NG + 1)
                tokens = resid[:, HT * (i % NG):HT * (i % NG) + HT, :]
                nc.vector.tensor_tensor(tokens, banks[COMBINE_BANKS[i]], tokens, ALU.add).then_inc(s_fin, 1)


def kernel(x, ctx_1024, L0_attn_Wq, L0_attn_bq, L0_attn_Wk, L0_attn_bk, L0_attn_Wv, L0_attn_bv, L0_attn_Wo, L0_attn_bo,
           L0_xattn_Wq, L0_xattn_Wk, L0_xattn_Wv, L0_xattn_bv, L0_xattn_Wo, L0_xattn_bo,
           L0_ffn_router_w1, L0_ffn_router_w2, L0_ffn_w1, L0_ffn_w2, L0_ffn_w3):
    import concourse.bacc as bacc
    from concourse.bass_utils import run_bass_kernel_spmd

    consts, masks = constants()
    square = [L0_attn_Wq, L0_attn_Wk, L0_attn_Wv, L0_attn_Wo, L0_xattn_Wq, L0_xattn_Wk, L0_xattn_Wv, L0_xattn_Wo]
    weights = np.stack([np.asarray(w).T for w in square] + [np.asarray(L0_ffn_router_w1)], 1)
    rows = np.stack([np.asarray(r) for r in (L0_attn_bv, L0_attn_bo, L0_xattn_bv, L0_xattn_bo)])
    w3 = np.asarray(L0_ffn_w3).reshape(E, MT, 128, D).transpose(0, 2, 1, 3).reshape(E, 128, MT * D)
    expert_w = np.concatenate([np.asarray(L0_ffn_w1), np.asarray(L0_ffn_w2), w3], 2)
    arrays = {
        "x": np.asarray(x),
        "ctx_t": np.asarray(ctx_1024).reshape(NG, HT * S, D).transpose(2, 0, 1),
        "consts": consts,
        "masks": masks,
        "weights": weights,
        "bias_cols": np.stack([np.asarray(L0_attn_bq), np.asarray(L0_attn_bk)], 1),
        "bias_rows": np.broadcast_to(rows, (128, 4, 128)),
        "rw2": np.asarray(L0_ffn_router_w2),
        "expert_w": expert_w,
    }
    arrays = {k: np.ascontiguousarray(v) for k, v in arrays.items()}
    nc = bacc.Bacc("TRN2", target_bir_lowering=False, num_devices=1)
    aps = {k: nc.dram_tensor(k, v.shape, mybir.dt.from_np(v.dtype), kind="ExternalInput").ap() for k, v in arrays.items()}
    out = nc.dram_tensor("out", (B, S, D), mybir.dt.float32, kind="ExternalOutput").ap()
    scratch = nc.dram_tensor("scratch", (2, 128, 2, HT * S), mybir.dt.float32, kind="Internal").ap()
    decoder_kernel(nc, **aps, scratch=scratch, out=out)
    return run_bass_kernel_spmd(nc, [arrays], core_ids=[0]).results[0]["out"]
```
